# Optimizing a Trainium2 kernel written in Bass

```python
import numpy as np
import jax
import jax.numpy as jnp

def _softmax(x, axis=-1):
    return jax.nn.softmax(x, axis=axis)
def _gelu(x):
    return jax.nn.gelu(x, approximate=True)
def _silu(x):
    return jax.nn.silu(x)
def _sigmoid(x):
    return jax.nn.sigmoid(x)
def _layernorm(x, axis=-1, eps=1e-5):
    m = jnp.mean(x, axis=axis, keepdims=True)
    v = jnp.var(x, axis=axis, keepdims=True)
    return (x - m) / jnp.sqrt(v + eps)
def _scatter_add(tgt, idx, src, axis=0):
    return tgt.at[idx].add(src)
def _segment_sum(src, seg, n):
    return jax.ops.segment_sum(src, seg, n)

kernel_name = 'mk_conv_seq_d1_conv_nchw256_3c3301'

def setup_inputs(seed: int = 0):
    np.random.seed(seed)
    _w = jnp.asarray
    def _rec_inputs():
        import jax
        import jax.numpy as jnp
        _gk = jax.random.key(seed)
        x = -0.0002074 + 1 * jax.random.normal(jax.random.fold_in(_gk, 1), (48, 256, 128, 17), jnp.float32)
        return x
    x = _rec_inputs()
    def _L0_conv_setup():
        import jax, jax.numpy as jnp
        import numpy as np
        N, C, T, V = (48, 256, 128, 17)
        REL, BR, NSUB, KS = (32, 64, 3, 5)
        DILATIONS = (1, 2)

        def _conv1x1(w, b, x):
            return jnp.einsum('oc,nctv->notv', w, x) + b[:, None, None]

        def _tconv(x, w, b, d):
            pad = (KS + (KS - 1) * (d - 1) - 1) // 2
            y = jax.lax.conv_general_dilated(x, w[..., None], (1, 1), ((pad, pad), (0, 0)), rhs_dilation=(d, 1), dimension_numbers=('NCHW', 'OIHW', 'NCHW'))
            return y + b[None, :, None, None]

        def _maxpool_t(x):
            return jax.lax.reduce_window(x, -jnp.inf, jax.lax.max, (1, 1, 3, 1), (1, 1, 1, 1), ((0, 0), (0, 0), (1, 1), (0, 0)))

        def _forward(x, A, alpha, g_c1w, g_c1b, g_c2w, g_c2b, g_c3w, g_c3b, g_rw, g_rb, gbn_s, gbn_b, br_w1, br_b1, br_s1, br_bb1, br_w2, br_b2, br_s2, br_bb2, mp_w1, mp_b1, mp_s1, mp_bb1, mp_s2, mp_bb2, p_w, p_b, p_s, p_bb):
            xm = x.mean(axis=2)

            def subset(Ai, c1w, c1b, c2w, c2b, c3w, c3b, rw, rb):
                inp = _conv1x1(rw, rb, x)
                x1 = jnp.einsum('rc,ncv->nrv', c1w, xm) + c1b[:, None]
                x2 = jnp.einsum('rc,ncv->nrv', c2w, xm) + c2b[:, None]
                m = jnp.tanh(x1[:, :, :, None] - x2[:, :, None, :])
                Af = jnp.einsum('or,nruv->nouv', c3w, m) + c3b[:, None, None]
                Af = Af * alpha[0] + Ai[None, None]
                return jnp.einsum('ncuv,nctv->nctu', Af, inp)
            y = jax.vmap(subset)(A, g_c1w, g_c1b, g_c2w, g_c2b, g_c3w, g_c3b, g_rw, g_rb).sum(0)
            y = jax.nn.relu(gbn_s[:, None, None] * y + gbn_b[:, None, None] + x)
            outs = []
            for k, d in enumerate(DILATIONS):
                h = jax.nn.relu(br_s1[k][:, None, None] * _conv1x1(br_w1[k], br_b1[k], y) + br_bb1[k][:, None, None])
                h = _tconv(h, br_w2[k], br_b2[k], d)
                outs.append(br_s2[k][:, None, None] * h + br_bb2[k][:, None, None])
            h = jax.nn.relu(mp_s1[:, None, None] * _conv1x1(mp_w1, mp_b1, y) + mp_bb1[:, None, None])
            h = _maxpool_t(h)
            outs.append(mp_s2[:, None, None] * h + mp_bb2[:, None, None])
            outs.append(p_s[:, None, None] * _conv1x1(p_w, p_b, y) + p_bb[:, None, None])
            out = jnp.concatenate(outs, axis=1)
            return jax.nn.relu(out + x)
        key = jax.random.key(seed)
        keys = iter(jax.random.split(key, 64))
        r = lambda *s: jax.random.normal(next(keys), s, jnp.float32)
        return {'x': r(N, C, T, V), 'A': 0.2 * r(NSUB, V, V), 'alpha': jnp.array([0.5], jnp.float32), 'g_c1w': 0.05 * r(NSUB, REL, C), 'g_c1b': 0.01 * r(NSUB, REL), 'g_c2w': 0.05 * r(NSUB, REL, C), 'g_c2b': 0.01 * r(NSUB, REL), 'g_c3w': 0.05 * r(NSUB, C, REL), 'g_c3b': 0.01 * r(NSUB, C), 'g_rw': 0.05 * r(NSUB, C, C), 'g_rb': 0.01 * r(NSUB, C), 'gbn_s': 1.0 + 0.1 * r(C), 'gbn_b': 0.05 * r(C), 'br_w1': 0.05 * r(2, BR, C), 'br_b1': 0.01 * r(2, BR), 'br_s1': 1.0 + 0.1 * r(2, BR), 'br_bb1': 0.05 * r(2, BR), 'br_w2': 0.05 * r(2, BR, BR, KS), 'br_b2': 0.01 * r(2, BR), 'br_s2': 1.0 + 0.1 * r(2, BR), 'br_bb2': 0.05 * r(2, BR), 'mp_w1': 0.05 * r(BR, C), 'mp_b1': 0.01 * r(BR), 'mp_s1': 1.0 + 0.1 * r(BR), 'mp_bb1': 0.05 * r(BR), 'mp_s2': 1.0 + 0.1 * r(BR), 'mp_bb2': 0.05 * r(BR), 'p_w': 0.05 * r(BR, C), 'p_b': 0.01 * r(BR), 'p_s': 1.0 + 0.1 * r(BR), 'p_bb': 0.05 * r(BR)}
    _L0_conv_all = _L0_conv_setup()
    _L0_conv_in = {k: v for k, v in _L0_conv_all.items() if k in ('A', 'alpha', 'g_c1w', 'g_c1b', 'g_c2w', 'g_c2b', 'g_c3w', 'g_c3b', 'g_rw', 'g_rb', 'gbn_s', 'gbn_b', 'br_w1', 'br_b1', 'br_s1', 'br_bb1', 'br_w2', 'br_b2', 'br_s2', 'br_bb2', 'mp_w1', 'mp_b1', 'mp_s1', 'mp_bb1', 'mp_s2', 'mp_bb2', 'p_w', 'p_b', 'p_s', 'p_bb', )}
    del _L0_conv_all

    return {
        "x": x,
        "L0_conv_A": _L0_conv_in["A"],
        "L0_conv_alpha": _L0_conv_in["alpha"],
        "L0_conv_g_c1w": _L0_conv_in["g_c1w"],
        "L0_conv_g_c1b": _L0_conv_in["g_c1b"],
        "L0_conv_g_c2w": _L0_conv_in["g_c2w"],
        "L0_conv_g_c2b": _L0_conv_in["g_c2b"],
        "L0_conv_g_c3w": _L0_conv_in["g_c3w"],
        "L0_conv_g_c3b": _L0_conv_in["g_c3b"],
        "L0_conv_g_rw": _L0_conv_in["g_rw"],
        "L0_conv_g_rb": _L0_conv_in["g_rb"],
        "L0_conv_gbn_s": _L0_conv_in["gbn_s"],
        "L0_conv_gbn_b": _L0_conv_in["gbn_b"],
        "L0_conv_br_w1": _L0_conv_in["br_w1"],
        "L0_conv_br_b1": _L0_conv_in["br_b1"],
        "L0_conv_br_s1": _L0_conv_in["br_s1"],
        "L0_conv_br_bb1": _L0_conv_in["br_bb1"],
        "L0_conv_br_w2": _L0_conv_in["br_w2"],
        "L0_conv_br_b2": _L0_conv_in["br_b2"],
        "L0_conv_br_s2": _L0_conv_in["br_s2"],
        "L0_conv_br_bb2": _L0_conv_in["br_bb2"],
        "L0_conv_mp_w1": _L0_conv_in["mp_w1"],
        "L0_conv_mp_b1": _L0_conv_in["mp_b1"],
        "L0_conv_mp_s1": _L0_conv_in["mp_s1"],
        "L0_conv_mp_bb1": _L0_conv_in["mp_bb1"],
        "L0_conv_mp_s2": _L0_conv_in["mp_s2"],
        "L0_conv_mp_bb2": _L0_conv_in["mp_bb2"],
        "L0_conv_p_w": _L0_conv_in["p_w"],
        "L0_conv_p_b": _L0_conv_in["p_b"],
        "L0_conv_p_s": _L0_conv_in["p_s"],
        "L0_conv_p_bb": _L0_conv_in["p_bb"],
    }

def reference(x, L0_conv_A, L0_conv_alpha, L0_conv_g_c1w, L0_conv_g_c1b, L0_conv_g_c2w, L0_conv_g_c2b, L0_conv_g_c3w, L0_conv_g_c3b, L0_conv_g_rw, L0_conv_g_rb, L0_conv_gbn_s, L0_conv_gbn_b, L0_conv_br_w1, L0_conv_br_b1, L0_conv_br_s1, L0_conv_br_bb1, L0_conv_br_w2, L0_conv_br_b2, L0_conv_br_s2, L0_conv_br_bb2, L0_conv_mp_w1, L0_conv_mp_b1, L0_conv_mp_s1, L0_conv_mp_bb1, L0_conv_mp_s2, L0_conv_mp_bb2, L0_conv_p_w, L0_conv_p_b, L0_conv_p_s, L0_conv_p_bb):
    import jax
    import jax.numpy as jnp
    def _L0_conv_ref(x, A, alpha, g_c1w, g_c1b, g_c2w, g_c2b, g_c3w, g_c3b, g_rw, g_rb, gbn_s, gbn_b, br_w1, br_b1, br_s1, br_bb1, br_w2, br_b2, br_s2, br_bb2, mp_w1, mp_b1, mp_s1, mp_bb1, mp_s2, mp_bb2, p_w, p_b, p_s, p_bb):
        import jax, jax.numpy as jnp
        import numpy as np
        N, C, T, V = (48, 256, 128, 17)
        REL, BR, NSUB, KS = (32, 64, 3, 5)
        DILATIONS = (1, 2)

        def _conv1x1(w, b, x):
            return jnp.einsum('oc,nctv->notv', w, x) + b[:, None, None]

        def _tconv(x, w, b, d):
            pad = (KS + (KS - 1) * (d - 1) - 1) // 2
            y = jax.lax.conv_general_dilated(x, w[..., None], (1, 1), ((pad, pad), (0, 0)), rhs_dilation=(d, 1), dimension_numbers=('NCHW', 'OIHW', 'NCHW'))
            return y + b[None, :, None, None]

        def _maxpool_t(x):
            return jax.lax.reduce_window(x, -jnp.inf, jax.lax.max, (1, 1, 3, 1), (1, 1, 1, 1), ((0, 0), (0, 0), (1, 1), (0, 0)))

        def _forward(x, A, alpha, g_c1w, g_c1b, g_c2w, g_c2b, g_c3w, g_c3b, g_rw, g_rb, gbn_s, gbn_b, br_w1, br_b1, br_s1, br_bb1, br_w2, br_b2, br_s2, br_bb2, mp_w1, mp_b1, mp_s1, mp_bb1, mp_s2, mp_bb2, p_w, p_b, p_s, p_bb):
            xm = x.mean(axis=2)

            def subset(Ai, c1w, c1b, c2w, c2b, c3w, c3b, rw, rb):
                inp = _conv1x1(rw, rb, x)
                x1 = jnp.einsum('rc,ncv->nrv', c1w, xm) + c1b[:, None]
                x2 = jnp.einsum('rc,ncv->nrv', c2w, xm) + c2b[:, None]
                m = jnp.tanh(x1[:, :, :, None] - x2[:, :, None, :])
                Af = jnp.einsum('or,nruv->nouv', c3w, m) + c3b[:, None, None]
                Af = Af * alpha[0] + Ai[None, None]
                return jnp.einsum('ncuv,nctv->nctu', Af, inp)
            y = jax.vmap(subset)(A, g_c1w, g_c1b, g_c2w, g_c2b, g_c3w, g_c3b, g_rw, g_rb).sum(0)
            y = jax.nn.relu(gbn_s[:, None, None] * y + gbn_b[:, None, None] + x)
            outs = []
            for k, d in enumerate(DILATIONS):
                h = jax.nn.relu(br_s1[k][:, None, None] * _conv1x1(br_w1[k], br_b1[k], y) + br_bb1[k][:, None, None])
                h = _tconv(h, br_w2[k], br_b2[k], d)
                outs.append(br_s2[k][:, None, None] * h + br_bb2[k][:, None, None])
            h = jax.nn.relu(mp_s1[:, None, None] * _conv1x1(mp_w1, mp_b1, y) + mp_bb1[:, None, None])
            h = _maxpool_t(h)
            outs.append(mp_s2[:, None, None] * h + mp_bb2[:, None, None])
            outs.append(p_s[:, None, None] * _conv1x1(p_w, p_b, y) + p_bb[:, None, None])
            out = jnp.concatenate(outs, axis=1)
            return jax.nn.relu(out + x)
        return _forward(x, A, alpha, g_c1w, g_c1b, g_c2w, g_c2b, g_c3w, g_c3b, g_rw, g_rb, gbn_s, gbn_b, br_w1, br_b1, br_s1, br_bb1, br_w2, br_b2, br_s2, br_bb2, mp_w1, mp_b1, mp_s1, mp_bb1, mp_s2, mp_bb2, p_w, p_b, p_s, p_bb)

    def _gn(v, G=32, eps=1e-5):
        B_, C_, H_, W_ = v.shape
        g = v.reshape(B_, G, C_ // G, H_, W_)
        m = jnp.mean(g, axis=(2, 3, 4), keepdims=True)
        s = jnp.var(g, axis=(2, 3, 4), keepdims=True)
        return ((g - m) / jnp.sqrt(s + eps)).reshape(v.shape)

    def _ln_c(v, eps=1e-6):
        m = jnp.mean(v, axis=1, keepdims=True)
        s = jnp.var(v, axis=1, keepdims=True)
        return (v - m) / jnp.sqrt(s + eps)

    def _ln_t(v, eps=1e-5):
        m = jnp.mean(v, axis=-1, keepdims=True)
        s = jnp.var(v, axis=-1, keepdims=True)
        return (v - m) / jnp.sqrt(s + eps)

    def _to_tokens(v):
        B_, C_, H_, W_ = v.shape
        return v.reshape(B_, C_, H_ * W_).transpose(0, 2, 1)
    def _from_tokens(t, like):
        B_, C_, H_, W_ = like.shape
        return t.transpose(0, 2, 1).reshape(B_, C_, H_, W_)

    x = _L0_conv_ref(x, L0_conv_A, L0_conv_alpha, L0_conv_g_c1w, L0_conv_g_c1b, L0_conv_g_c2w, L0_conv_g_c2b, L0_conv_g_c3w, L0_conv_g_c3b, L0_conv_g_rw, L0_conv_g_rb, L0_conv_gbn_s, L0_conv_gbn_b, L0_conv_br_w1, L0_conv_br_b1, L0_conv_br_s1, L0_conv_br_bb1, L0_conv_br_w2, L0_conv_br_b2, L0_conv_br_s2, L0_conv_br_bb2, L0_conv_mp_w1, L0_conv_mp_b1, L0_conv_mp_s1, L0_conv_mp_bb1, L0_conv_mp_s2, L0_conv_mp_bb2, L0_conv_p_w, L0_conv_p_b, L0_conv_p_s, L0_conv_p_bb)
    return x


_drawn_inputs = setup_inputs


def setup_inputs(seed=0):
    import zlib

    import numpy as np

    out = dict(_drawn_inputs(seed))
    spreads = {}
    factors = {'L0_conv_g_c1w': 2.903,
     'L0_conv_g_c1b': 22.825,
     'L0_conv_g_c2w': 2.901,
     'L0_conv_g_c2b': 8.0,
     'L0_conv_g_c3b': 5.771,
     'L0_conv_g_rb': 8.0,
     'L0_conv_gbn_b': 3.374,
     'L0_conv_br_b1': 8.0,
     'L0_conv_br_bb1': 3.591,
     'L0_conv_br_b2': 8.0,
     'L0_conv_mp_b1': 8.0,
     'L0_conv_mp_bb1': 3.0,
     'L0_conv_mp_bb2': 2.696,
     'L0_conv_p_b': 8.0,
     'L0_conv_p_bb': 3.544}
    for name, (base, spread) in spreads.items():
        noise = np.random.default_rng([zlib.crc32(name.encode()), seed]).standard_normal(out[name].shape)
        drawn = base * np.exp(spread * noise) if base else spread * noise
        out[name] = jnp.asarray(drawn.astype(out[name].dtype))
    for name, factor in factors.items():
        out[name] = (out[name] * factor).astype(out[name].dtype)
    return out
```

```python
from contextlib import ExitStack

import concourse.bass as bass
from concourse import mybir

F32 = mybir.dt.float32
F32R = mybir.dt.float32r
ALU = mybir.AluOpType
ACT = mybir.ActivationFunctionType
AX = mybir.AxisListType

P = 128
T = 128
V = 17
TV = T * V
CB = 2
SUB = 3
REL = 32
KS = 5
BLK = SUB * CB
KA = SUB * V
KP = 2 * KA
KM = SUB * REL + SUB + 1
MW = 2 * KA

TCH = 28
HCH = [(t0, min(TCH, T - t0)) for t0 in range(0, T, TCH)]
UCH = [(u0, min(4, V - u0)) for u0 in range(0, V, 4)]
NK = len(HCH)
assert NK == len(UCH) == 5
XW = TCH * V

SEG = T // 2 + 4
LH = 2 * SEG

G_PROJ = 0
TR_OF = [2 + t0 // 4 for t0, _ in HCH]
G_TOP = 2 + T // 4
UPG = 2
N_TOP = -(-V // UPG)
G_S2 = G_TOP + N_TOP
SW = 4 * V
PPG = 512 // SW
N_S2 = -(-P // PPG)
G_END = G_S2 + N_S2
assert G_END % 2 == 0
TRB = G_END // 2


def some(count):
    return not isinstance(count, int) or count > 0


def groups_before(g, bank):
    return (g + 1 - bank) // 2


AHEAD = 2
AHEAD_BLOCKS = AHEAD * BLK - 1


def ahead_blocks(j):
    def until(x):
        return x * AHEAD_BLOCKS // (N_S2 - 1)
    return range(until(j - 1), until(j)) if j else range(0)


V_GS, V_GB, V_RB, V_S1, V_B1, V_BB1, V_B2, V_BB2 = 0, 2, 4, 10, 11, 12, 13, 14
V_SM, V_BM, V_BBM, V_SO, V_BO, V_BBO, V_C1, V_C2, V_AL, V_S2 = 15, 16, 17, 18, 19, 20, 21, 22, 23, 24
NV = 25
D_IN, D_H, D_A, D_M, D_B, D_D = 0, 6, 7, 8, 9, 10
ND = 11


def build(nc, x, rw, c12, c3, atop, ind, w3, w2, s2row, ident_in, vecs_in, out):
    NS = x.shape[0]
    NX = 3
    assert NS % NX == 0 and NS >= 2 * NX
    ctx = ExitStack()
    with ctx:
        def sb(name, shape, dt=F32):
            return ctx.enter_context(nc.sbuf_tensor(name, shape, dt))

        def sem(name):
            return ctx.enter_context(nc.semaphore(name))

        xb = [sb(f"x{i}", [P, CB, TV]) for i in range(NX)]
        xh = [sb(f"x_high{i}", [P, CB, XW], F32R) for i in range(2)]
        xl = [sb(f"x_low{i}", [P, CB, XW], F32R) for i in range(2)]
        inp = [sb(f"inp{i}", [P, TCH, KP]) for i in range(2)]
        inpT = sb("inpT", [P, P, T])
        top = sb("top", [P, (P + 1) * 2 * V])
        yh = sb("y_high", [P, CB, 512], F32R)
        yl = sb("y_low", [P, CB, 512], F32R)
        hf = sb("h", [P, 4, LH])
        hh = sb("h_high", [P, 4, LH], F32R)
        hl = sb("h_low", [P, 4, LH], F32R)
        mf = sb("pool_in", [64, 4, T + 2])
        sumA = sb("sumA", [P, 512])
        rwh = sb("rw_high", [P, CB, BLK * P], F32R)
        rwl = sb("rw_low", [P, CB, BLK * P], F32R)
        w3h = sb("w3_high", [P, CB, 2 * P], F32R)
        w3l = sb("w3_low", [P, CB, 2 * P], F32R)
        w2h = sb("w2_high", [P, KS, P], F32R)
        w2l = sb("w2_low", [P, KS, P], F32R)
        mbd = sb("tanh_blocks", [KM, KA + V * MW])
        c3T = sb("c3T", [KM, CB * P])
        c12T = sb("c12T", [P, CB, 2 * SUB * REL])
        ident = sb("ident", [P, P])
        vec = sb("vec", [P, NV])
        der = sb("derived", [P, ND])
        xm = sb("xm", [P, CB, V])
        proj2 = sb("proj2", [SUB * REL, V])
        diff = sb("diff", [SUB * REL, V * V])

        ps_inp = [ctx.enter_context(nc.psum_tensor(f"ps_inp{i}", [P, 512], F32)) for i in range(2)]
        ps_tr = [ctx.enter_context(nc.psum_tensor(f"ps_tr{i}", [P, 512], F32)) for i in range(2)]
        ps_y = [ctx.enter_context(nc.psum_tensor(f"ps_y{i}", [P, 512], F32)) for i in range(2)]
        ps_h = ctx.enter_context(nc.psum_tensor("ps_h", [P, 512], F32))
        ps_m = ctx.enter_context(nc.psum_tensor("ps_m", [P, 512], F32))

        stage = inpT[:, :, :].rearrange("p a b -> p (a b)")
        st_rw = stage[:, 0:CB * BLK * P]
        st_w3 = stage[:, 2048:2048 + CB * 2 * P]
        st_w2 = stage[:, 3072:3072 + KS * P]
        st_s2 = stage[:, 4096:4096 + P]

        consts_loaded = sem("consts_loaded")
        blocks_cleared = sem("blocks_cleared")
        rows_loaded = sem("rows_loaded")
        setup_step = sem("setup_step")
        setup_done = sem("setup_done")
        x_loaded = [sem(f"x_loaded{i}") for i in range(NX)]
        out_stored = [sem(f"out_stored{i}") for i in range(NX)]
        xh_ready = sem("xh_ready")
        xl_ready = sem("xl_ready")
        inp_full = [sem(f"inp_full{i}") for i in range(2)]
        inp_taken = [sem(f"inp_taken{i}") for i in range(2)]
        tr_full = [sem(f"tr_full{i}") for i in range(2)]
        tr_taken = [sem(f"tr_taken{i}") for i in range(2)]
        xm_ready = sem("xm_ready")
        tanh_ready = sem("tanh_ready")
        y_full = [sem(f"y_full{i}") for i in range(2)]
        y_added = [sem(f"y_added{i}") for i in range(2)]
        yh_ready = [sem(f"yh_ready{i}") for i in range(2)]
        y_split = [sem(f"y_split{i}") for i in range(2)]
        h_full = sem("h_full")
        m_full = sem("m_full")
        hf_ready = sem("hf_ready")
        mf_ready = sem("mf_ready")
        hh_ready = sem("hh_ready")
        hl_ready = sem("hl_ready")
        conv_full = sem("conv_full")
        pool_step = sem("pool_step")
        sumA_ready = sem("sumA_ready")
        sumB_ready = sem("sumB_ready")
        outA_done = sem("outA_done")
        outB_done = sem("outB_done")
        block = ctx.enter_context(nc.Block())

        def all_samples(eng, step):
            step(0, 0, 0, True, False, True)
            step(1, 0, 1, True, True, True)
            with eng.Fori(0, NS // NX - 1) as i:
                step(i * NX + 2, i, 2, True, True, True)
                step(i * NX + 3, i + 1, 0, True, True, True)
                step(i * NX + 4, i + 1, 1, True, True, True)
            step(NS - 1, NS // NX - 1, 2, True, True, False)
            step(NS, NS // NX, 0, False, True, False)

        def joints(buf, lo, hi, cb, u0, us):
            return buf[lo:hi, cb, :].rearrange("c (t v) -> c v t", v=V)[:, u0:u0 + us, :]

        def following(h, r):
            return (h + 1, 0) if r == NX - 1 else (h, r + 1)

        @block.sync
        def _(sp):
            def load(n, r):
                for cb in range(CB):
                    sp.dma_start(xb[r][:, cb, :], x[n, cb * P:(cb + 1) * P, :]).then_inc(x_loaded[r], 16)

            def finish(n, h, r, again):
                sp.wait_ge(outA_done, n * NK + NK)
                sp.wait_ge(outB_done, n * NK + NK)
                for cb in range(CB):
                    sp.dma_start(out[n, cb * P:(cb + 1) * P, :], xb[r][:, cb, :]).then_inc(out_stored[r], 16)
                sp.wait_ge(out_stored[r], h * 32 + 32)
                if again:
                    load(n + NX, r)

            sp.dma_start(st_rw, rw).then_inc(consts_loaded, 16)
            sp.dma_start(vec[:, :], vecs_in).then_inc(consts_loaded, 16)
            load(0, 0)
            sp.dma_start(c12T[:, :, :], c12).then_inc(consts_loaded, 16)
            sp.dma_start(ident[:, :], ident_in).then_inc(consts_loaded, 16)
            sp.dma_start(c3T[:, :], c3).then_inc(consts_loaded, 16)
            sp.dma_start(st_w3, w3).then_inc(consts_loaded, 16)
            sp.dma_start(st_w2, w2).then_inc(consts_loaded, 16)
            sp.dma_start(st_s2, s2row.partition_broadcast(P)).then_inc(consts_loaded, 16)
            sp.wait_ge(blocks_cleared, 1)
            for lo, hi, src in ((SUB * REL, KM - 1, ind), (KM - 1, KM, atop)):
                rows = mbd[lo:hi, :]
                dst = bass.AP(mbd, rows.offset + KA, [rows.ap[0], [MW, V], [1, KA]])
                sp.dma_start(dst, src).then_inc(rows_loaded, 16)
            load(1, 1)
            load(2, 2)
            with sp.Fori(0, NS // NX - 1) as i:
                for r in range(NX):
                    finish(i * NX + r, i, r, True)
            for r in range(NX):
                finish(NS - NX + r, NS // NX - 1, r, False)

        @block.gpsimd
        def _(pool):
            def x_low(n, r, k):
                t0, ts = HCH[k]
                pool.wait_ge(xh_ready, n * NK + k + 1)
                nc.gpsimd.tensor_tensor(xl[k % 2][:, :, 0:ts * V], xb[r][:, :, t0 * V:(t0 + ts) * V],
                                        xh[k % 2][:, :, 0:ts * V].bitcast(F32), ALU.subtract).then_inc(xl_ready, 1)

            def h_low(m, k):
                us = UCH[k][1]
                pool.wait_ge(hh_ready, m * NK + k + 1)
                nc.gpsimd.tensor_tensor(hl[:, 0:us, :], hf[:, 0:us, :], hh[:, 0:us, :].bitcast(F32),
                                        ALU.subtract).then_inc(hl_ready, 1)

            def step(n, h, r, head, tail, ahead):
                h1, r1 = following(h, r)
                if head:
                    x_low(n, r, NK - 1)
                for k in range(3):
                    if tail:
                        h_low(n - 1, k)
                if ahead:
                    x_low(n + 1, r1, 0)
                    x_low(n + 1, r1, 1)
                for k in range(3, NK):
                    if tail:
                        h_low(n - 1, k)
                if ahead:
                    x_low(n + 1, r1, 2)
                    x_low(n + 1, r1, 3)

            for k in range(NK - 1):
                x_low(0, 0, k)
            all_samples(pool, step)

        @block.scalar
        def _(act):
            def x_high(n, h, r, k):
                t0, ts = HCH[k]
                if k == 0:
                    act.wait_ge(x_loaded[r], h * 32 + 32)
                nc.scalar.activation(xh[k % 2][:, :, 0:ts * V], xb[r][:, :, t0 * V:(t0 + ts) * V],
                                     ACT.Copy).then_inc(xh_ready, 1)

            def take_inp(n, k, b):
                ts = HCH[k][1]
                cb = b // SUB
                act.wait_ge(inp_full[b % 2], n * 3 * NK + 3 * k + b // 2 + 1)
                nc.scalar.activation(inp[k % 2][:, 0:ts, b * V:(b + 1) * V],
                                     ps_inp[b % 2][:, 0:ts * V].rearrange("c (t v) -> c t v", v=V), ACT.Identity,
                                     bias=der[:, D_IN + b:D_IN + b + 1],
                                     scale=vec[:, V_GS + cb:V_GS + cb + 1]).then_inc(inp_taken[b % 2], 1)

            def take_tr(n, k, j):
                t0 = HCH[k][0] + 4 * j
                g = TR_OF[k] + j
                if g % 2 == 0:
                    act.wait_ge(tr_full[0], n * TRB + g // 2 + 1)
                    nc.scalar.activation(inpT[0:KP, :, t0:t0 + 4], ps_tr[0][0:KP, :].rearrange("k (t p) -> k p t", t=4),
                                         ACT.Copy).then_inc(tr_taken[0], 1)

            def take_top(n, j):
                g = G_TOP + j
                us = min(UPG, V - j * UPG)
                act.wait_ge(tr_full[g % 2], n * TRB + g // 2 + 1)
                nc.scalar.activation(
                    top[0:KP, 0:P * 2 * V].rearrange("k (p c u) -> k u c p", c=2, u=V)[:, j * UPG:j * UPG + us],
                    ps_tr[g % 2][0:KP, 0:us * 2 * P].rearrange("k (u c p) -> k u c p", c=2, u=us), ACT.Copy
                ).then_inc(tr_taken[g % 2], 1)

            def tanh(n):
                act.wait_ge(tr_taken[0], n * TRB + G_PROJ // 2 + 1)
                for i in range(SUB):
                    rows = mbd[REL * i:REL * (i + 1), :]
                    dst = bass.AP(mbd, rows.offset + KA + V * i, [rows.ap[0], [MW, V], [1, V]])
                    ins = nc.scalar.activation(dst, diff[REL * i:REL * (i + 1), :].rearrange("r (u v) -> r u v", v=V),
                                               ACT.Tanh, bias=der[REL * i:REL * (i + 1), D_D:D_D + 1], scale=1.0 / T)
                ins.then_inc(tanh_ready, 1)

            def y_high(m, k, cb):
                w = UCH[k][1] * T
                act.wait_ge(y_added[cb], m * NK + k + 1)
                nc.scalar.activation(yh[:, cb, 0:w], ps_y[cb][:, 0:w], ACT.Relu).then_inc(yh_ready[cb], 1)

            def hidden_m(m, k):
                us = UCH[k][1]
                act.wait_ge(m_full, m * NK + k + 1)
                nc.scalar.activation(mf[:, 0:us, 1:T + 1], ps_m[0:64, 0:us * T].rearrange("c (u t) -> c u t", t=T),
                                     ACT.Relu, bias=der[0:64, D_M:D_M + 1],
                                     scale=vec[0:64, V_SM:V_SM + 1]).then_inc(mf_ready, 1)

            def hidden_h(m, k):
                us = UCH[k][1]
                act.wait_ge(h_full, m * NK + k + 1)
                nc.scalar.activation(
                    bass.AP(hf, 2, [hf[0:64, :, :].ap[0], [LH, us], [SEG - 2, 2], [1, SEG - 2]]),
                    bass.AP(ps_h, 0, [ps_h[0:64, :].ap[0], [T, us], [SEG - 6, 2], [1, SEG - 2]]), ACT.Relu,
                    bias=der[0:64, D_H:D_H + 1], scale=vec[0:64, V_S1:V_S1 + 1])
                src = ps_h[64:P, 0:us * T].rearrange("c (u q s) -> c u s q", s=2, u=us)
                dst = hf[64:P, 0:us, :].rearrange("c u (s q) -> c u s q", s=2)[:, :, :, 2:2 + T // 2]
                nc.scalar.activation(dst, src, ACT.Relu, bias=der[64:P, D_H:D_H + 1],
                                     scale=vec[64:P, V_S1:V_S1 + 1]).then_inc(hf_ready, 1)

            def outA(m, k, buf):
                u0, us = UCH[k]
                act.wait_ge(sumA_ready, m * NK + k + 1)
                nc.scalar.activation(joints(buf, 0, P, 0, u0, us),
                                     sumA[:, 0:us * T].rearrange("c (u t) -> c u t", t=T), ACT.Relu,
                                     bias=der[:, D_A:D_A + 1]).then_inc(outA_done, 1)

            def outB(m, k, buf):
                u0, us = UCH[k]
                act.wait_ge(sumB_ready, m * NK + k + 1)
                nc.scalar.activation(joints(buf, 0, P, 1, u0, us),
                                     ps_m[:, 0:us * T].rearrange("c (u t) -> c u t", t=T), ACT.Relu,
                                     bias=der[:, D_B:D_B + 1]).then_inc(outB_done, 1)

            def take_s2(n, j):
                g = G_S2 + j
                pairs = min(PPG, P - j * PPG)
                c0 = j * PPG * 2 * V
                act.wait_ge(tr_full[g % 2], n * TRB + g // 2 + 1)
                nc.scalar.activation(top[:, c0:c0 + pairs * 2 * V].rearrange("t (i w) -> t i w", w=2 * V),
                                     ps_tr[g % 2][:, 0:pairs * SW].rearrange("t (i w) -> t i w", w=SW)[:, :, 0:2 * V],
                                     ACT.Copy).then_inc(tr_taken[g % 2], 1)

            def step(n, h, r, head, tail, ahead):
                m = n - 1
                buf = xb[(r - 1) % NX]
                h1, r1 = following(h, r)
                for k in range(NK - 1):
                    if tail and k >= 2:
                        outA(m, k - 2, buf)
                    for j in range(7):
                        if head:
                            take_tr(n, k, j)
                        if tail and k and j == 2:
                            hidden_m(m, k - 1)
                        if tail and k and j == 4:
                            hidden_h(m, k - 1)
                    if k < 3:
                        if head:
                            for b in range(3):
                                take_inp(n, k + AHEAD, b)
                        if tail:
                            y_high(m, k, 0)
                        if head:
                            take_inp(n, k + AHEAD, 3)
                        if tail:
                            y_high(m, k, 1)
                        if head:
                            take_inp(n, k + AHEAD, 4)
                            take_inp(n, k + AHEAD, 5)
                            if k == 0:
                                x_high(n, h, r, NK - 1)
                                tanh(n)
                        if tail and k:
                            outB(m, k - 1, buf)
                if tail:
                    y_high(m, 3, 0)
                    y_high(m, 3, 1)
                if head:
                    for j in range(HCH[4][1] // 4):
                        take_tr(n, 4, j)
                if tail:
                    outB(m, 2, buf)
                if ahead:
                    x_high(n + 1, h1, r1, 0)
                    x_high(n + 1, h1, r1, 1)
                if tail:
                    hidden_m(m, 3)
                    hidden_h(m, 3)
                    outA(m, 2, buf)
                    y_high(m, 4, 0)
                    y_high(m, 4, 1)
                for j in range(0, N_TOP, 2):
                    if head:
                        take_top(n, j)
                    if tail and j == 4:
                        outB(m, 3, buf)
                if tail:
                    outA(m, 3, buf)
                    hidden_m(m, 4)
                    hidden_h(m, 4)
                    outB(m, 4, buf)
                for j in range(N_S2):
                    if head:
                        take_s2(n, j)
                    if tail and j == 8:
                        outA(m, 4, buf)
                    if ahead:
                        for b in ahead_blocks(j):
                            take_inp(n + 1, b // BLK, b % BLK)
                            if b == BLK - 1:
                                x_high(n + 1, h1, r1, 2)
                if ahead:
                    take_inp(n + 1, 1, BLK - 1)
                    x_high(n + 1, h1, r1, 3)

            x_high(0, 0, 0, 0)
            x_high(0, 0, 0, 1)
            act.wait_ge(setup_done, 1)
            for k in range(AHEAD):
                for b in range(BLK):
                    take_inp(0, k, b)
                x_high(0, 0, 0, 2 + k)
            all_samples(act, step)

        @block.vector
        def _(dve):
            steps = [0]

            def then(ins):
                steps[0] += 1
                ins.then_inc(setup_step, 1)
                dve.wait_ge(setup_step, steps[0])

            nc.vector.memset(mbd[:, :], 0.0).then_inc(blocks_cleared, 1)
            nc.vector.memset(hf[:, :, :], 0.0)
            nc.vector.memset(top[:, P * 2 * V:], 0.0)
            nc.vector.memset(mf[:, :, :], 0.0)
            dve.wait_ge(consts_loaded, 8 * 16)
            dve.wait_ge(rows_loaded, 32)

            def high_low(h, l, src):
                then(nc.vector.tensor_copy(h, src))
                nc.vector.tensor_tensor(l, src, h.bitcast(F32), ALU.subtract)

            high_low(rwh[:, :, :].rearrange("p a b -> p (a b)"), rwl[:, :, :].rearrange("p a b -> p (a b)"), st_rw)
            high_low(w3h[:, :, :].rearrange("p a b -> p (a b)"), w3l[:, :, :].rearrange("p a b -> p (a b)"), st_w3)
            for k in range(KS):
                ins = nc.vector.tensor_tensor(st_w2[:, k * P:(k + 1) * P], st_w2[:, k * P:(k + 1) * P], st_s2, ALU.mult)
            then(ins)
            high_low(w2h[:, :, :].rearrange("p a b -> p (a b)"), w2l[:, :, :].rearrange("p a b -> p (a b)"), st_w2)
            nc.vector.tensor_scalar(c3T[0:KM - 1, :], c3T[0:KM - 1, :], vec[0:KM - 1, V_AL:V_AL + 1], None, ALU.mult)
            for cb in range(CB):
                nc.vector.tensor_scalar(der[:, D_IN + SUB * cb:D_IN + SUB * cb + SUB],
                                        vec[:, V_RB + SUB * cb:V_RB + SUB * cb + SUB],
                                        vec[:, V_GS + cb:V_GS + cb + 1], None, ALU.mult)

            def fused_bias(dst, s, b, bb):
                nc.vector.scalar_tensor_tensor(der[:, dst:dst + 1], vec[:, b:b + 1], vec[:, s:s + 1],
                                               vec[:, bb:bb + 1], ALU.mult, ALU.add)

            fused_bias(D_H, V_S1, V_B1, V_BB1)
            fused_bias(D_A, V_S2, V_B2, V_BB2)
            fused_bias(D_M, V_SM, V_BM, V_BBM)
            fused_bias(D_B, V_SO, V_BO, V_BBO)
            nc.vector.tensor_tensor(der[:, D_D:D_D + 1], vec[:, V_C1:V_C1 + 1], vec[:, V_C2:V_C2 + 1],
                                    ALU.subtract).then_inc(setup_done, 1)

            def mean(n, h, r):
                dve.wait_ge(x_loaded[r], h * 32 + 32)
                nc.vector.tensor_reduce(xm[:, :, :], xb[r][:, :, :].rearrange("p c (t v) -> p c v t", v=V),
                                        AX.X, ALU.add).then_inc(xm_ready, 1)

            def differences(n):
                dve.wait_ge(tr_full[1], n * TRB + G_PROJ // 2 + 1)
                nc.vector.tensor_copy(proj2[:, :], ps_tr[1][0:SUB * REL, 0:V]).then_inc(tr_taken[1], 1)
                dve.wait_ge(tr_taken[1], n * TRB + G_PROJ // 2 + 1)
                nc.vector.tensor_tensor(diff[:, :].rearrange("r (u v) -> r u v", v=V),
                                        ps_tr[0][0:SUB * REL, 0:V].unsqueeze(2).to_broadcast([SUB * REL, V, V]),
                                        proj2[:, :].unsqueeze(1).to_broadcast([SUB * REL, V, V]),
                                        ALU.subtract).then_inc(tr_taken[0], 1)

            def take_tr(n, k):
                for j in range(HCH[k][1] // 4):
                    t0 = HCH[k][0] + 4 * j
                    g = TR_OF[k] + j
                    if g % 2:
                        dve.wait_ge(tr_full[1], n * TRB + g // 2 + 1)
                        nc.vector.tensor_copy(inpT[0:KP, :, t0:t0 + 4],
                                              ps_tr[1][0:KP, :].rearrange("k (t p) -> k p t", t=4)
                                              ).then_inc(tr_taken[1], 1)

            def take_top(n, j):
                g = G_TOP + j
                us = min(UPG, V - j * UPG)
                dve.wait_ge(tr_full[g % 2], n * TRB + g // 2 + 1)
                nc.vector.tensor_copy(
                    top[0:KP, 0:P * 2 * V].rearrange("k (p c u) -> k u c p", c=2, u=V)[:, j * UPG:j * UPG + us],
                    ps_tr[g % 2][0:KP, 0:us * 2 * P].rearrange("k (u c p) -> k u c p", c=2, u=us)
                ).then_inc(tr_taken[g % 2], 1)

            def add_x(m, k, cb, buf):
                u0, us = UCH[k]
                y = ps_y[cb][:, 0:us * T].rearrange("c (u t) -> c u t", t=T)
                dve.wait_ge(y_full[cb], m * NK + k + 1)
                nc.vector.scalar_tensor_tensor(y, y, vec[:, V_GB + cb:V_GB + cb + 1], joints(buf, 0, P, cb, u0, us),
                                               ALU.add, ALU.add).then_inc(y_added[cb], 1)

            def y_low(m, k, cb):
                w = UCH[k][1] * T
                dve.wait_ge(yh_ready[cb], m * NK + k + 1)
                nc.vector.scalar_tensor_tensor(yl[:, cb, 0:w], ps_y[cb][:, 0:w], 0.0, yh[:, cb, 0:w].bitcast(F32),
                                               ALU.max, ALU.subtract).then_inc(y_split[cb], 1)

            def y_chunk(m, k, buf):
                for cb in range(CB):
                    add_x(m, k, cb, buf)
                for cb in range(CB):
                    y_low(m, k, cb)

            def h_high(m, k):
                us = UCH[k][1]
                dve.wait_ge(hf_ready, m * NK + k + 1)
                nc.vector.tensor_copy(hh[:, 0:us, :], hf[:, 0:us, :]).then_inc(hh_ready, 1)

            def pooled(m, k, buf, part=None):
                u0, us = UCH[k]
                low = ps_m[0:64, 0:us * T].rearrange("c (u t) -> c u t", t=T)
                high = ps_m[64:P, 0:us * T].rearrange("c (u t) -> c u t", t=T)
                if part != 1:
                    dve.wait_ge(mf_ready, m * NK + k + 1)
                    nc.vector.tensor_tensor(low, mf[:, 0:us, 0:T], mf[:, 0:us, 1:T + 1], ALU.max).then_inc(pool_step, 1)
                    nc.vector.scalar_tensor_tensor(high, high, vec[64:P, V_SO:V_SO + 1],
                                                   joints(buf, 64, P, 1, u0, us), ALU.mult, ALU.add)
                if part != 0:
                    dve.wait_ge(pool_step, m * 2 * NK + 2 * k + 1)
                    nc.vector.tensor_tensor(low, low, mf[:, 0:us, 2:T + 2], ALU.max).then_inc(pool_step, 1)
                    dve.wait_ge(pool_step, m * 2 * NK + 2 * k + 2)
                    nc.vector.scalar_tensor_tensor(low, low, vec[0:64, V_SO:V_SO + 1], joints(buf, 0, 64, 1, u0, us),
                                                   ALU.mult, ALU.add).then_inc(sumB_ready, 1)

            def convolved(m, k, buf):
                u0, us = UCH[k]
                w = us * T
                dve.wait_ge(conv_full, m * NK + k + 1)
                if some(m * NK + k):
                    dve.wait_ge(outA_done, m * NK + k)
                nc.vector.tensor_tensor(sumA[0:64, 0:w].rearrange("c (u t) -> c u t", t=T),
                                        ps_h[0:64, 0:w].rearrange("c (u t) -> c u t", t=T),
                                        joints(buf, 0, 64, 0, u0, us), ALU.add)
                nc.vector.tensor_tensor(
                    sumA[64:P, 0:w].rearrange("c (u q s) -> c u s q", s=2, u=us),
                    ps_h[64:P, 0:w].rearrange("c (u s q) -> c u s q", s=2, u=us),
                    joints(buf, 64, P, 0, u0, us).rearrange("c u (q s) -> c u s q", s=2),
                    ALU.add).then_inc(sumA_ready, 1)

            def step(n, h, r, head, tail, ahead):
                m = n - 1
                buf = xb[(r - 1) % NX]
                h1, r1 = following(h, r)
                for k in range(3):
                    if tail and k >= 2:
                        convolved(m, k - 2, buf)
                    if head:
                        take_tr(n, k)
                    if tail and k:
                        h_high(m, k - 1)
                        pooled(m, k - 1, buf)
                    if tail:
                        y_chunk(m, k, buf)
                if tail:
                    convolved(m, 1, buf)
                if head:
                    take_tr(n, 3)
                if tail:
                    h_high(m, 2)
                    y_chunk(m, 3, buf)
                if head:
                    take_tr(n, 4)
                if tail:
                    pooled(m, 2, buf)
                    convolved(m, 2, buf)
                    h_high(m, 3)
                    y_chunk(m, 4, buf)
                for j in range(1, N_TOP, 2):
                    if head:
                        take_top(n, j)
                    if tail and j < 5:
                        pooled(m, 3, buf, j // 2)
                if tail:
                    convolved(m, 3, buf)
                    h_high(m, 4)
                    pooled(m, 4, buf)
                    convolved(m, 4, buf)
                if ahead:
                    mean(n + 1, h1, r1)
                    differences(n + 1)

            mean(0, 0, 0)
            differences(0)
            all_samples(dve, step)

        @block.tensor
        def _(pe):
            def three(out, w, a, first, last):
                nc.tensor.matmul(out, w[0], a[0], start=first, stop=False)
                nc.tensor.matmul(out, w[0], a[1], start=False, stop=False)
                return nc.tensor.matmul(out, w[1], a[0], start=False, stop=last)

            def s1_half(n, k, b, kb):
                w = HCH[k][1] * V
                if b == 0 and kb == 0:
                    pe.wait_ge(xl_ready, n * NK + k + 1)
                before = n * 3 * NK + 3 * k + b // 2
                if kb == 0 and some(before):
                    pe.wait_ge(inp_taken[b % 2], before)
                cols = slice(b * P, (b + 1) * P)
                ins = three(ps_inp[b % 2][:, 0:w], (rwh[:, kb, cols], rwl[:, kb, cols]),
                            (xh[k % 2][:, kb, 0:w], xl[k % 2][:, kb, 0:w]), kb == 0, kb == CB - 1)
                if kb == CB - 1:
                    ins.then_inc(inp_full[b % 2], 1)

            def s1(n, k, b):
                for kb in range(CB):
                    s1_half(n, k, b, kb)

            def tr1(n, k, j):
                g = TR_OF[k] + j
                if j == 0:
                    for b in range(2):
                        pe.wait_ge(inp_taken[b], n * 3 * NK + 3 * (k + 1))
                pe.wait_ge(tr_taken[g % 2], n * TRB + g // 2)
                for t in range(4):
                    ins = nc.tensor.transpose(ps_tr[g % 2][0:KP, t * P:(t + 1) * P], inp[k % 2][:, 4 * j + t, :],
                                              ident[:, :])
                ins.then_inc(tr_full[g % 2], 1)

            def projections(n):
                pe.wait_ge(xm_ready, n + 1)
                for s in range(2):
                    g = G_PROJ + s
                    if some(n * TRB):
                        pe.wait_ge(tr_taken[g % 2], n * TRB)
                    for kb in range(CB):
                        ins = nc.tensor.matmul(ps_tr[g % 2][0:SUB * REL, 0:V],
                                               c12T[:, kb, s * SUB * REL:(s + 1) * SUB * REL], xm[:, kb, :],
                                               start=kb == 0, stop=kb == CB - 1)
                    ins.then_inc(tr_full[g % 2], 1)

            def topologies(n):
                pe.wait_ge(tanh_ready, n + 1)
                for j in range(N_TOP):
                    g = G_TOP + j
                    pe.wait_ge(tr_taken[g % 2], n * TRB + g // 2)
                    for uu in range(min(UPG, V - j * UPG)):
                        u = j * UPG + uu
                        for c in range(2):
                            w0 = u * MW + (KA if c == 0 else 0)
                            ins = nc.tensor.matmul(ps_tr[g % 2][0:KP, (2 * uu + c) * P:(2 * uu + c + 1) * P],
                                                   mbd[:, w0:w0 + KP], c3T[:, c * P:(c + 1) * P],
                                                   start=True, stop=True)
                    ins.then_inc(tr_full[g % 2], 1)

            def s2(n, j):
                g = G_S2 + j
                if j == 0:
                    for b in range(2):
                        pe.wait_ge(tr_taken[b], n * TRB + groups_before(G_S2, b))
                else:
                    pe.wait_ge(tr_taken[g % 2], n * TRB + g // 2)
                for i in range(min(PPG, P - j * PPG)):
                    p = j * PPG + i
                    ins = nc.tensor.matmul(ps_tr[g % 2][:, i * SW:(i + 1) * SW], inpT[0:KP, p, :],
                                           top[0:KP, p * 2 * V:p * 2 * V + SW], start=True, stop=True)
                ins.then_inc(tr_full[g % 2], 1)

            def tr2(m, k):
                u0, us = UCH[k]
                if k == 0:
                    for b in range(2):
                        pe.wait_ge(tr_taken[b], m * TRB + TRB)
                for cb in range(CB):
                    if some(m * NK + k):
                        pe.wait_ge(y_split[cb], m * NK + k)
                    for j in range(us):
                        src = top[:, 0:P * 2 * V].rearrange("t (p c u) -> t c u p", c=2, u=V)[:, cb, u0 + j, :]
                        ins = nc.tensor.transpose(ps_y[cb][:, j * T:(j + 1) * T], src, ident[:, :])
                    ins.then_inc(y_full[cb], 1)

            def s3_half(m, k, blk, kb):
                w = UCH[k][1] * T
                if blk and kb == 0:
                    for cb in range(CB):
                        pe.wait_ge(y_split[cb], m * NK + k + 1)
                if kb == 0 and some(m * NK + k):
                    pe.wait_ge(outB_done if blk else sumA_ready, m * NK + k)
                cols = slice(blk * P, (blk + 1) * P)
                ins = three((ps_m if blk else ps_h)[:, 0:w], (w3h[:, kb, cols], w3l[:, kb, cols]),
                            (yh[:, kb, 0:w], yl[:, kb, 0:w]), kb == 0, kb == CB - 1)
                if kb == CB - 1:
                    ins.then_inc(m_full if blk else h_full, 1)

            S3 = ((1, 0), (1, 1), (0, 0), (0, 1))

            def conv(m, k):
                us = UCH[k][1]
                pe.wait_ge(hl_ready, m * NK + k + 1)
                for tap in range(KS):
                    def at(h):
                        return h[:, 0:us, :].rearrange("c u (s q) -> c u s q", s=2)[:, :, :, tap:tap + T // 2]
                    ins = three(ps_h[:, 0:us * T], (w2h[:, tap, :], w2l[:, tap, :]), (at(hh), at(hl)),
                                tap == 0, tap == KS - 1)
                ins.then_inc(conv_full, 1)

            def step(n, h, r, head, tail, ahead):
                m = n - 1
                for k in range(NK - 1):
                    for j in range(7):
                        if head:
                            tr1(n, k, j)
                        if tail and k and 1 <= j < 5:
                            s3_half(m, k - 1, *S3[j - 1])
                    if head and k < 3:
                        for b in range(3):
                            s1(n, k + AHEAD, b)
                    if tail:
                        tr2(m, k)
                    if head and k < 3:
                        for b in range(3, BLK):
                            s1(n, k + AHEAD, b)
                    if head and k == 3:
                        for j in range(HCH[4][1] // 4):
                            tr1(n, 4, j)
                    if tail and k:
                        conv(m, k - 1)
                if tail:
                    for half in S3:
                        s3_half(m, 3, *half)
                    tr2(m, 4)
                if head:
                    topologies(n)
                if tail:
                    conv(m, 3)
                    for half in S3:
                        s3_half(m, 4, *half)
                for j in range(N_S2):
                    if head:
                        s2(n, j)
                    if tail and j == 4:
                        conv(m, 4)
                    if ahead:
                        for b in ahead_blocks(j):
                            s1(n + 1, b // BLK, b % BLK)
                if ahead:
                    projections(n + 1)
                    s1(n + 1, 1, BLK - 1)

            pe.wait_ge(setup_done, 1)
            for k in range(AHEAD):
                for b in range(BLK):
                    s1(0, k, b)
            projections(0)
            all_samples(pe, step)


def kernel(**a):
    import numpy as np
    import concourse.bacc as bacc
    from concourse.bass_utils import run_bass_kernel_spmd

    a = {k.replace("L0_conv_", ""): np.asarray(v) for k, v in a.items()}
    N, C = a["x"].shape[:2]
    f = np.float32
    z64 = np.zeros(64, f)

    def kblocks(w):
        return np.ascontiguousarray(w.reshape(CB, P, -1).transpose(1, 0, 2).reshape(P, -1))

    rw = a["g_rw"].reshape(SUB, CB, P, C).transpose(3, 1, 0, 2).reshape(C, BLK * P)
    w3 = np.concatenate([a["br_w1"].reshape(2 * 64, C), a["mp_w1"], a["p_w"]], 0).T
    w2 = np.zeros((P, KS, P), f)
    for k in range(2):
        w2[64 * k:64 * k + 64, :, 64 * k:64 * k + 64] = a["br_w2"][k].transpose(1, 2, 0)
    c12 = np.concatenate([a["g_c1w"].reshape(SUB * REL, C), a["g_c2w"].reshape(SUB * REL, C)], 0).T
    c3 = np.concatenate([a["g_c3w"].transpose(0, 2, 1).reshape(SUB * REL, C), a["g_c3b"], np.ones((1, C), f)], 0)
    atop = np.ascontiguousarray(a["A"].transpose(1, 0, 2)).reshape(1, V, KA)
    ind = np.ascontiguousarray(np.broadcast_to(np.repeat(np.eye(SUB, dtype=f), V, 1)[:, None, :], (SUB, V, KA)))
    vecs = np.zeros((P, NV), f)
    vecs[:, V_GS:V_GS + 2] = a["gbn_s"].reshape(CB, P).T
    vecs[:, V_GB:V_GB + 2] = a["gbn_b"].reshape(CB, P).T
    vecs[:, V_RB:V_RB + 6] = a["g_rb"].reshape(SUB, CB, P).transpose(2, 1, 0).reshape(P, BLK)
    for col, v in ((V_S1, a["br_s1"].reshape(P)), (V_B1, a["br_b1"].reshape(P)), (V_BB1, a["br_bb1"].reshape(P)),
                   (V_S2, a["br_s2"].reshape(P)), (V_B2, a["br_b2"].reshape(P)), (V_BB2, a["br_bb2"].reshape(P)),
                   (V_SM, np.concatenate([a["mp_s1"], z64])), (V_BM, np.concatenate([a["mp_b1"], z64])),
                   (V_BBM, np.concatenate([a["mp_bb1"], z64])), (V_SO, np.concatenate([a["mp_s2"], a["p_s"]])),
                   (V_BO, np.concatenate([z64, a["p_b"]])), (V_BBO, np.concatenate([a["mp_bb2"], a["p_bb"]]))):
        vecs[:, col] = v
    vecs[0:SUB * REL, V_C1] = a["g_c1b"].reshape(-1)
    vecs[0:SUB * REL, V_C2] = a["g_c2b"].reshape(-1)
    vecs[:, V_AL] = a["alpha"][0]
    arrays = {
        "x": np.ascontiguousarray(a["x"].reshape(N, C, TV)), "rw": kblocks(rw), "c12": kblocks(c12), "c3": c3,
        "atop": atop, "ind": ind, "w3": kblocks(w3), "w2": w2.reshape(P, KS * P),
        "s2row": np.ascontiguousarray(a["br_s2"].reshape(P)), "ident": np.eye(P, dtype=f), "vecs": vecs,
    }
    nc = bacc.Bacc("TRN2", target_bir_lowering=False, num_devices=1,
                   dynamic_dma_scratch_size=1024)
    args, ins = [], {}
    for name, arr in arrays.items():
        arr = np.ascontiguousarray(arr)
        ins[f"in_{name}"] = arr
        args.append(nc.dram_tensor(f"in_{name}", arr.shape, mybir.dt.from_np(arr.dtype), kind="ExternalInput").ap())
    args.append(nc.dram_tensor("out", (N, C, TV), F32, kind="ExternalOutput").ap())
    args[2] = args[2].rearrange("p (k o) -> p k o", k=CB)
    build(nc, *args)
    r = run_bass_kernel_spmd(nc, [ins], core_ids=[0])
    return r.results[0]["out"].reshape(N, C, T, V)
```

```python
from contextlib import ExitStack

import concourse.bass as bass
from concourse import mybir

F32 = mybir.dt.float32
F32R = mybir.dt.float32r
ALU = mybir.AluOpType
ACT = mybir.ActivationFunctionType
AX = mybir.AxisListType

P = 128
T = 128
V = 17
TV = T * V
CB = 2
SUB = 3
REL = 32
KS = 5
BLK = SUB * CB
KA = SUB * V
KP = 2 * KA
KM = SUB * REL + SUB + 1
MW = 2 * KA

TCH = 28
HCH = [(t0, min(TCH, T - t0)) for t0 in range(0, T, TCH)]
UCH = [(u0, min(4, V - u0)) for u0 in range(0, V, 4)]
NK = len(HCH)
assert NK == len(UCH) == 5
XW = TCH * V

SEG = T // 2 + 4
LH = 2 * SEG

G_PROJ = 0
TR_OF = [2 + t0 // 4 for t0, _ in HCH]
G_TOP = 2 + T // 4
UPG = 2
N_TOP = -(-V // UPG)
G_S2 = G_TOP + N_TOP
SW = 4 * V
PPG = 512 // SW
N_S2 = -(-P // PPG)
G_END = G_S2 + N_S2
assert G_END % 2 == 0
TRB = G_END // 2


def some(count):
    return not isinstance(count, int) or count > 0


def groups_before(g, bank):
    return (g + 1 - bank) // 2


AHEAD = 2
AHEAD_TOP = 2
AHEAD_S2 = AHEAD * BLK - 2


def ahead_blocks(j):
    def until(x):
        return AHEAD_TOP + x * (AHEAD_S2 - AHEAD_TOP) // (N_S2 - 1)
    return range(until(j - 1), until(j)) if j else range(0)


V_GS, V_GB, V_RB, V_S1, V_B1, V_BB1, V_B2, V_BB2 = 0, 2, 4, 10, 11, 12, 13, 14
V_SM, V_BM, V_BBM, V_SO, V_BO, V_BBO, V_C1, V_C2, V_AL, V_S2 = 15, 16, 17, 18, 19, 20, 21, 22, 23, 24
NV = 25
D_IN, D_H, D_A, D_M, D_B, D_D = 0, 6, 7, 8, 9, 10
ND = 11


def build(nc, x, rw, c12, c3, atop, ind, w3, w2, s2row, ident_in, vecs_in, out):
    NS = x.shape[0]
    NX = 3
    assert NS % NX == 0 and NS >= 2 * NX
    ctx = ExitStack()
    with ctx:
        def sb(name, shape, dt=F32):
            return ctx.enter_context(nc.sbuf_tensor(name, shape, dt))

        def sem(name):
            return ctx.enter_context(nc.semaphore(name))

        xb = [sb(f"x{i}", [P, CB, TV]) for i in range(NX)]
        xh = [sb(f"x_high{i}", [P, CB, XW], F32R) for i in range(2)]
        xl = [sb(f"x_low{i}", [P, CB, XW], F32R) for i in range(2)]
        inp = [sb(f"inp{i}", [P, TCH, KP]) for i in range(2)]
        inpT = sb("inpT", [P, P, T])
        top = sb("top", [P, (P + 1) * 2 * V])
        yh = sb("y_high", [P, CB, 512], F32R)
        yl = sb("y_low", [P, CB, 512], F32R)
        hf = sb("h", [P, 4, LH])
        hh = sb("h_high", [P, 4, LH], F32R)
        hl = sb("h_low", [P, 4, LH], F32R)
        mf = sb("pool_in", [64, 4, T + 2])
        sumA = sb("sumA", [P, 512])
        rwh = sb("rw_high", [P, CB, BLK * P], F32R)
        rwl = sb("rw_low", [P, CB, BLK * P], F32R)
        w3h = sb("w3_high", [P, CB, 2 * P], F32R)
        w3l = sb("w3_low", [P, CB, 2 * P], F32R)
        w2h = sb("w2_high", [P, KS, P], F32R)
        w2l = sb("w2_low", [P, KS, P], F32R)
        mbd = sb("tanh_blocks", [KM, KA + V * MW])
        c3T = sb("c3T", [KM, CB * P])
        c12T = sb("c12T", [P, CB, 2 * SUB * REL])
        ident = sb("ident", [P, P])
        vec = sb("vec", [P, NV])
        der = sb("derived", [P, ND])
        xm = sb("xm", [P, CB, V])
        proj2 = sb("proj2", [SUB * REL, V])
        diff = sb("diff", [SUB * REL, V * V])

        ps_inp = [ctx.enter_context(nc.psum_tensor(f"ps_inp{i}", [P, 512], F32)) for i in range(2)]
        ps_tr = [ctx.enter_context(nc.psum_tensor(f"ps_tr{i}", [P, 512], F32)) for i in range(2)]
        ps_y = [ctx.enter_context(nc.psum_tensor(f"ps_y{i}", [P, 512], F32)) for i in range(2)]
        ps_h = ctx.enter_context(nc.psum_tensor("ps_h", [P, 512], F32))
        ps_m = ctx.enter_context(nc.psum_tensor("ps_m", [P, 512], F32))

        stage = inpT[:, :, :].rearrange("p a b -> p (a b)")
        st_rw = stage[:, 0:CB * BLK * P]
        st_w3 = stage[:, 2048:2048 + CB * 2 * P]
        st_w2 = stage[:, 3072:3072 + KS * P]
        st_s2 = stage[:, 4096:4096 + P]

        consts_loaded = sem("consts_loaded")
        blocks_cleared = sem("blocks_cleared")
        rows_loaded = sem("rows_loaded")
        setup_step = sem("setup_step")
        setup_done = sem("setup_done")
        x_loaded = [sem(f"x_loaded{i}") for i in range(NX)]
        out_stored = [sem(f"out_stored{i}") for i in range(NX)]
        xh_ready = sem("xh_ready")
        xl_ready = sem("xl_ready")
        inp_full = [sem(f"inp_full{i}") for i in range(2)]
        inp_taken = [sem(f"inp_taken{i}") for i in range(2)]
        tr_full = [sem(f"tr_full{i}") for i in range(2)]
        tr_taken = [sem(f"tr_taken{i}") for i in range(2)]
        xm_ready = sem("xm_ready")
        tanh_ready = sem("tanh_ready")
        y_full = [sem(f"y_full{i}") for i in range(2)]
        y_added = [sem(f"y_added{i}") for i in range(2)]
        yh_ready = [sem(f"yh_ready{i}") for i in range(2)]
        y_split = [sem(f"y_split{i}") for i in range(2)]
        h_full = sem("h_full")
        m_full = sem("m_full")
        hf_ready = sem("hf_ready")
        mf_ready = sem("mf_ready")
        hh_ready = sem("hh_ready")
        hl_ready = sem("hl_ready")
        conv_full = sem("conv_full")
        pool_step = sem("pool_step")
        sumA_ready = sem("sumA_ready")
        sumB_ready = sem("sumB_ready")
        outA_done = sem("outA_done")
        outB_done = sem("outB_done")
        block = ctx.enter_context(nc.Block())

        def all_samples(eng, step):
            step(0, 0, 0, True, False, True)
            step(1, 0, 1, True, True, True)
            with eng.Fori(0, NS // NX - 1) as i:
                step(i * NX + 2, i, 2, True, True, True)
                step(i * NX + 3, i + 1, 0, True, True, True)
                step(i * NX + 4, i + 1, 1, True, True, True)
            step(NS - 1, NS // NX - 1, 2, True, True, False)
            step(NS, NS // NX, 0, False, True, False)

        def joints(buf, lo, hi, cb, u0, us):
            return buf[lo:hi, cb, :].rearrange("c (t v) -> c v t", v=V)[:, u0:u0 + us, :]

        def following(h, r):
            return (h + 1, 0) if r == NX - 1 else (h, r + 1)

        @block.sync
        def _(sp):
            def load(n, r):
                for cb in range(CB):
                    sp.dma_start(xb[r][:, cb, :], x[n, cb * P:(cb + 1) * P, :]).then_inc(x_loaded[r], 16)

            def finish(n, h, r, again):
                sp.wait_ge(outA_done, n * NK + NK)
                sp.wait_ge(outB_done, n * NK + NK)
                for cb in range(CB):
                    sp.dma_start(out[n, cb * P:(cb + 1) * P, :], xb[r][:, cb, :]).then_inc(out_stored[r], 16)
                sp.wait_ge(out_stored[r], h * 32 + 32)
                if again:
                    load(n + NX, r)

            sp.dma_start(st_rw, rw).then_inc(consts_loaded, 16)
            sp.dma_start(vec[:, :], vecs_in).then_inc(consts_loaded, 16)
            load(0, 0)
            sp.dma_start(c12T[:, :, :], c12).then_inc(consts_loaded, 16)
            sp.dma_start(ident[:, :], ident_in).then_inc(consts_loaded, 16)
            sp.dma_start(c3T[:, :], c3).then_inc(consts_loaded, 16)
            sp.dma_start(st_w3, w3).then_inc(consts_loaded, 16)
            sp.dma_start(st_w2, w2).then_inc(consts_loaded, 16)
            sp.dma_start(st_s2, s2row.partition_broadcast(P)).then_inc(consts_loaded, 16)
            sp.wait_ge(blocks_cleared, 1)
            for lo, hi, src in ((SUB * REL, KM - 1, ind), (KM - 1, KM, atop)):
                rows = mbd[lo:hi, :]
                dst = bass.AP(mbd, rows.offset + KA, [rows.ap[0], [MW, V], [1, KA]])
                sp.dma_start(dst, src).then_inc(rows_loaded, 16)
            load(1, 1)
            load(2, 2)
            with sp.Fori(0, NS // NX - 1) as i:
                for r in range(NX):
                    finish(i * NX + r, i, r, True)
            for r in range(NX):
                finish(NS - NX + r, NS // NX - 1, r, False)

        @block.gpsimd
        def _(pool):
            def x_low(n, r, k):
                t0, ts = HCH[k]
                pool.wait_ge(xh_ready, n * NK + k + 1)
                nc.gpsimd.tensor_tensor(xl[k % 2][:, :, 0:ts * V], xb[r][:, :, t0 * V:(t0 + ts) * V],
                                        xh[k % 2][:, :, 0:ts * V].bitcast(F32), ALU.subtract).then_inc(xl_ready, 1)

            def h_low(m, k):
                us = UCH[k][1]
                pool.wait_ge(hh_ready, m * NK + k + 1)
                nc.gpsimd.tensor_tensor(hl[:, 0:us, :], hf[:, 0:us, :], hh[:, 0:us, :].bitcast(F32),
                                        ALU.subtract).then_inc(hl_ready, 1)

            def step(n, h, r, head, tail, ahead):
                h1, r1 = following(h, r)
                if head:
                    x_low(n, r, 3)
                    x_low(n, r, 4)
                for k in range(3):
                    if tail:
                        h_low(n - 1, k)
                if ahead:
                    x_low(n + 1, r1, 0)
                    x_low(n + 1, r1, 1)
                for k in range(3, NK):
                    if tail:
                        h_low(n - 1, k)
                if ahead:
                    x_low(n + 1, r1, 2)

            for k in range(3):
                x_low(0, 0, k)
            all_samples(pool, step)

        @block.scalar
        def _(act):
            def x_high(n, h, r, k):
                t0, ts = HCH[k]
                if k == 0:
                    act.wait_ge(x_loaded[r], h * 32 + 32)
                nc.scalar.activation(xh[k % 2][:, :, 0:ts * V], xb[r][:, :, t0 * V:(t0 + ts) * V],
                                     ACT.Copy).then_inc(xh_ready, 1)

            def take_inp(n, k, b):
                ts = HCH[k][1]
                cb = b // SUB
                act.wait_ge(inp_full[b % 2], n * 3 * NK + 3 * k + b // 2 + 1)
                nc.scalar.activation(inp[k % 2][:, 0:ts, b * V:(b + 1) * V],
                                     ps_inp[b % 2][:, 0:ts * V].rearrange("c (t v) -> c t v", v=V), ACT.Identity,
                                     bias=der[:, D_IN + b:D_IN + b + 1],
                                     scale=vec[:, V_GS + cb:V_GS + cb + 1]).then_inc(inp_taken[b % 2], 1)

            def take_tr(n, k, j):
                t0 = HCH[k][0] + 4 * j
                g = TR_OF[k] + j
                if g % 2 == 0:
                    act.wait_ge(tr_full[0], n * TRB + g // 2 + 1)
                    nc.scalar.activation(inpT[0:KP, :, t0:t0 + 4], ps_tr[0][0:KP, :].rearrange("k (t p) -> k p t", t=4),
                                         ACT.Copy).then_inc(tr_taken[0], 1)

            def take_top(n, j):
                g = G_TOP + j
                us = min(UPG, V - j * UPG)
                act.wait_ge(tr_full[g % 2], n * TRB + g // 2 + 1)
                nc.scalar.activation(
                    top[0:KP, 0:P * 2 * V].rearrange("k (p c u) -> k u c p", c=2, u=V)[:, j * UPG:j * UPG + us],
                    ps_tr[g % 2][0:KP, 0:us * 2 * P].rearrange("k (u c p) -> k u c p", c=2, u=us), ACT.Copy
                ).then_inc(tr_taken[g % 2], 1)

            def tanh(n):
                act.wait_ge(tr_taken[0], n * TRB + G_PROJ // 2 + 1)
                for i in range(SUB):
                    rows = mbd[REL * i:REL * (i + 1), :]
                    dst = bass.AP(mbd, rows.offset + KA + V * i, [rows.ap[0], [MW, V], [1, V]])
                    ins = nc.scalar.activation(dst, diff[REL * i:REL * (i + 1), :].rearrange("r (u v) -> r u v", v=V),
                                               ACT.Tanh, bias=der[REL * i:REL * (i + 1), D_D:D_D + 1], scale=1.0 / T)
                ins.then_inc(tanh_ready, 1)

            def y_high(m, k, cb):
                w = UCH[k][1] * T
                act.wait_ge(y_added[cb], m * NK + k + 1)
                nc.scalar.activation(yh[:, cb, 0:w], ps_y[cb][:, 0:w], ACT.Relu).then_inc(yh_ready[cb], 1)

            def hidden_m(m, k):
                us = UCH[k][1]
                act.wait_ge(m_full, m * NK + k + 1)
                nc.scalar.activation(mf[:, 0:us, 1:T + 1], ps_m[0:64, 0:us * T].rearrange("c (u t) -> c u t", t=T),
                                     ACT.Relu, bias=der[0:64, D_M:D_M + 1],
                                     scale=vec[0:64, V_SM:V_SM + 1]).then_inc(mf_ready, 1)

            def hidden_h(m, k):
                us = UCH[k][1]
                act.wait_ge(h_full, m * NK + k + 1)
                nc.scalar.activation(
                    bass.AP(hf, 2, [hf[0:64, :, :].ap[0], [LH, us], [SEG - 2, 2], [1, SEG - 2]]),
                    bass.AP(ps_h, 0, [ps_h[0:64, :].ap[0], [T, us], [SEG - 6, 2], [1, SEG - 2]]), ACT.Relu,
                    bias=der[0:64, D_H:D_H + 1], scale=vec[0:64, V_S1:V_S1 + 1])
                src = ps_h[64:P, 0:us * T].rearrange("c (u q s) -> c u s q", s=2, u=us)
                dst = hf[64:P, 0:us, :].rearrange("c u (s q) -> c u s q", s=2)[:, :, :, 2:2 + T // 2]
                nc.scalar.activation(dst, src, ACT.Relu, bias=der[64:P, D_H:D_H + 1],
                                     scale=vec[64:P, V_S1:V_S1 + 1]).then_inc(hf_ready, 1)

            def outA(m, k, buf):
                u0, us = UCH[k]
                act.wait_ge(sumA_ready, m * NK + k + 1)
                nc.scalar.activation(joints(buf, 0, P, 0, u0, us),
                                     sumA[:, 0:us * T].rearrange("c (u t) -> c u t", t=T), ACT.Relu,
                                     bias=der[:, D_A:D_A + 1]).then_inc(outA_done, 1)

            def outB(m, k, buf):
                u0, us = UCH[k]
                act.wait_ge(sumB_ready, m * NK + k + 1)
                nc.scalar.activation(joints(buf, 0, P, 1, u0, us),
                                     ps_m[:, 0:us * T].rearrange("c (u t) -> c u t", t=T), ACT.Relu,
                                     bias=der[:, D_B:D_B + 1]).then_inc(outB_done, 1)

            def take_s2(n, j):
                g = G_S2 + j
                pairs = min(PPG, P - j * PPG)
                c0 = j * PPG * 2 * V
                act.wait_ge(tr_full[g % 2], n * TRB + g // 2 + 1)
                nc.scalar.activation(top[:, c0:c0 + pairs * 2 * V].rearrange("t (i w) -> t i w", w=2 * V),
                                     ps_tr[g % 2][:, 0:pairs * SW].rearrange("t (i w) -> t i w", w=SW)[:, :, 0:2 * V],
                                     ACT.Copy).then_inc(tr_taken[g % 2], 1)

            def step(n, h, r, head, tail, ahead):
                m = n - 1
                buf = xb[(r - 1) % NX]
                h1, r1 = following(h, r)
                if head:
                    take_tr(n, 0, 0)
                    take_inp(n, 1, BLK - 1)
                    take_tr(n, 0, 2)
                    x_high(n, h, r, 3)
                    take_tr(n, 0, 4)
                    take_tr(n, 0, 6)
                    for b in range(3):
                        take_inp(n, 2, b)
                if tail:
                    y_high(m, 0, 0)
                if head:
                    take_inp(n, 2, 3)
                if tail:
                    y_high(m, 0, 1)
                if head:
                    take_inp(n, 2, 4)
                    take_inp(n, 2, 5)
                    x_high(n, h, r, 4)
                for k in range(1, 3):
                    if head:
                        for j in range(2):
                            take_tr(n, k, j)
                    if tail and k == 2:
                        outA(m, 0, buf)
                    if head:
                        take_tr(n, k, 2)
                    if tail:
                        hidden_m(m, k - 1)
                    if head:
                        take_tr(n, k, 3)
                        take_tr(n, k, 4)
                    if tail:
                        hidden_h(m, k - 1)
                    if head:
                        take_tr(n, k, 5)
                        take_tr(n, k, 6)
                        if k == 1:
                            act.wait_ge(tr_full[1], n * TRB + (TR_OF[1] + 6) // 2 + 1)
                        for b in range(3):
                            take_inp(n, k + 2, b)
                    if tail:
                        y_high(m, k, 0)
                    if head:
                        take_inp(n, k + 2, 3)
                    if tail:
                        y_high(m, k, 1)
                    if head and k == 1:
                        take_inp(n, 3, 4)
                        take_inp(n, 3, 5)
                        tanh(n)
                    if tail:
                        outB(m, k - 1, buf)
                if head:
                    take_tr(n, 3, 1)
                if tail:
                    outA(m, 1, buf)
                    hidden_m(m, 2)
                if head:
                    take_tr(n, 3, 3)
                if tail:
                    hidden_h(m, 2)
                if head:
                    take_tr(n, 3, 5)
                    take_inp(n, 4, 4)
                    take_inp(n, 4, 5)
                if ahead:
                    x_high(n + 1, h1, r1, 0)
                if head:
                    take_tr(n, 4, 0)
                if tail:
                    y_high(m, 3, 0)
                    y_high(m, 3, 1)
                if head:
                    take_tr(n, 4, 2)
                if ahead:
                    x_high(n + 1, h1, r1, 1)
                if head:
                    take_top(n, 0)
                if ahead:
                    take_inp(n + 1, 0, 0)
                if tail:
                    outB(m, 2, buf)
                if head:
                    take_top(n, 2)
                if tail:
                    outA(m, 2, buf)
                if head:
                    take_top(n, 4)
                if tail:
                    hidden_m(m, 3)
                if head:
                    take_top(n, 6)
                if tail:
                    hidden_h(m, 3)
                if head:
                    take_top(n, 8)
                if tail:
                    y_high(m, 4, 0)
                    y_high(m, 4, 1)
                if ahead:
                    take_inp(n + 1, 0, 1)
                for j in range(N_S2):
                    if head:
                        take_s2(n, j)
                    if ahead:
                        for b in ahead_blocks(j):
                            take_inp(n + 1, b // BLK, b % BLK)
                            if b == BLK - 1:
                                x_high(n + 1, h1, r1, 2)
                    if tail and j == 1:
                        outB(m, 3, buf)
                    if tail and j == 4:
                        outA(m, 3, buf)
                    if tail and j == 5:
                        hidden_m(m, 4)
                    if tail and j == 7:
                        hidden_h(m, 4)
                    if tail and j == 9:
                        outB(m, 4, buf)
                    if tail and j == 11:
                        outA(m, 4, buf)
                if ahead:
                    take_inp(n + 1, 1, 4)

            x_high(0, 0, 0, 0)
            x_high(0, 0, 0, 1)
            act.wait_ge(setup_done, 1)
            for b in range(AHEAD * BLK - 1):
                take_inp(0, b // BLK, b % BLK)
                if b == BLK - 1:
                    x_high(0, 0, 0, 2)
            all_samples(act, step)

        @block.vector
        def _(dve):
            steps = [0]

            def then(ins):
                steps[0] += 1
                ins.then_inc(setup_step, 1)
                dve.wait_ge(setup_step, steps[0])

            nc.vector.memset(mbd[:, :], 0.0).then_inc(blocks_cleared, 1)
            nc.vector.memset(hf[:, :, :], 0.0)
            nc.vector.memset(top[:, P * 2 * V:], 0.0)
            nc.vector.memset(mf[:, :, :], 0.0)
            dve.wait_ge(consts_loaded, 8 * 16)
            dve.wait_ge(rows_loaded, 32)

            def high_low(h, l, src):
                then(nc.vector.tensor_copy(h, src))
                nc.vector.tensor_tensor(l, src, h.bitcast(F32), ALU.subtract)

            high_low(rwh[:, :, :].rearrange("p a b -> p (a b)"), rwl[:, :, :].rearrange("p a b -> p (a b)"), st_rw)
            high_low(w3h[:, :, :].rearrange("p a b -> p (a b)"), w3l[:, :, :].rearrange("p a b -> p (a b)"), st_w3)
            for k in range(KS):
                ins = nc.vector.tensor_tensor(st_w2[:, k * P:(k + 1) * P], st_w2[:, k * P:(k + 1) * P], st_s2, ALU.mult)
            then(ins)
            high_low(w2h[:, :, :].rearrange("p a b -> p (a b)"), w2l[:, :, :].rearrange("p a b -> p (a b)"), st_w2)
            nc.vector.tensor_scalar(c3T[0:KM - 1, :], c3T[0:KM - 1, :], vec[0:KM - 1, V_AL:V_AL + 1], None, ALU.mult)
            for cb in range(CB):
                nc.vector.tensor_scalar(der[:, D_IN + SUB * cb:D_IN + SUB * cb + SUB],
                                        vec[:, V_RB + SUB * cb:V_RB + SUB * cb + SUB],
                                        vec[:, V_GS + cb:V_GS + cb + 1], None, ALU.mult)

            def fused_bias(dst, s, b, bb):
                nc.vector.scalar_tensor_tensor(der[:, dst:dst + 1], vec[:, b:b + 1], vec[:, s:s + 1],
                                               vec[:, bb:bb + 1], ALU.mult, ALU.add)

            fused_bias(D_H, V_S1, V_B1, V_BB1)
            fused_bias(D_A, V_S2, V_B2, V_BB2)
            fused_bias(D_M, V_SM, V_BM, V_BBM)
            fused_bias(D_B, V_SO, V_BO, V_BBO)
            nc.vector.tensor_tensor(der[:, D_D:D_D + 1], vec[:, V_C1:V_C1 + 1], vec[:, V_C2:V_C2 + 1],
                                    ALU.subtract).then_inc(setup_done, 1)

            def mean(n, h, r):
                dve.wait_ge(x_loaded[r], h * 32 + 32)
                nc.vector.tensor_reduce(xm[:, :, :], xb[r][:, :, :].rearrange("p c (t v) -> p c v t", v=V),
                                        AX.X, ALU.add).then_inc(xm_ready, 1)

            def differences(n):
                dve.wait_ge(tr_full[1], n * TRB + G_PROJ // 2 + 1)
                nc.vector.tensor_copy(proj2[:, :], ps_tr[1][0:SUB * REL, 0:V]).then_inc(tr_taken[1], 1)
                dve.wait_ge(tr_taken[1], n * TRB + G_PROJ // 2 + 1)
                nc.vector.tensor_tensor(diff[:, :].rearrange("r (u v) -> r u v", v=V),
                                        ps_tr[0][0:SUB * REL, 0:V].unsqueeze(2).to_broadcast([SUB * REL, V, V]),
                                        proj2[:, :].unsqueeze(1).to_broadcast([SUB * REL, V, V]),
                                        ALU.subtract).then_inc(tr_taken[0], 1)

            def take_tr(n, k, js=range(7)):
                for j in js:
                    t0 = HCH[k][0] + 4 * j
                    g = TR_OF[k] + j
                    if g % 2:
                        dve.wait_ge(tr_full[1], n * TRB + g // 2 + 1)
                        nc.vector.tensor_copy(inpT[0:KP, :, t0:t0 + 4],
                                              ps_tr[1][0:KP, :].rearrange("k (t p) -> k p t", t=4)
                                              ).then_inc(tr_taken[1], 1)

            def take_top(n, j):
                g = G_TOP + j
                us = min(UPG, V - j * UPG)
                dve.wait_ge(tr_full[g % 2], n * TRB + g // 2 + 1)
                nc.vector.tensor_copy(
                    top[0:KP, 0:P * 2 * V].rearrange("k (p c u) -> k u c p", c=2, u=V)[:, j * UPG:j * UPG + us],
                    ps_tr[g % 2][0:KP, 0:us * 2 * P].rearrange("k (u c p) -> k u c p", c=2, u=us)
                ).then_inc(tr_taken[g % 2], 1)

            def add_x(m, k, cb, buf):
                u0, us = UCH[k]
                y = ps_y[cb][:, 0:us * T].rearrange("c (u t) -> c u t", t=T)
                dve.wait_ge(y_full[cb], m * NK + k + 1)
                nc.vector.scalar_tensor_tensor(y, y, vec[:, V_GB + cb:V_GB + cb + 1], joints(buf, 0, P, cb, u0, us),
                                               ALU.add, ALU.add).then_inc(y_added[cb], 1)

            def y_low(m, k, cb):
                w = UCH[k][1] * T
                dve.wait_ge(yh_ready[cb], m * NK + k + 1)
                nc.vector.scalar_tensor_tensor(yl[:, cb, 0:w], ps_y[cb][:, 0:w], 0.0, yh[:, cb, 0:w].bitcast(F32),
                                               ALU.max, ALU.subtract).then_inc(y_split[cb], 1)

            def both_added(m, k, buf):
                for cb in range(CB):
                    add_x(m, k, cb, buf)

            def both_low(m, k):
                for cb in range(CB):
                    y_low(m, k, cb)

            def h_high(m, k):
                us = UCH[k][1]
                dve.wait_ge(hf_ready, m * NK + k + 1)
                nc.vector.tensor_copy(hh[:, 0:us, :], hf[:, 0:us, :]).then_inc(hh_ready, 1)

            def pooled(m, k, buf, part=None):
                u0, us = UCH[k]
                low = ps_m[0:64, 0:us * T].rearrange("c (u t) -> c u t", t=T)
                high = ps_m[64:P, 0:us * T].rearrange("c (u t) -> c u t", t=T)
                if part != 1:
                    dve.wait_ge(mf_ready, m * NK + k + 1)
                    nc.vector.tensor_tensor(low, mf[:, 0:us, 0:T], mf[:, 0:us, 1:T + 1], ALU.max).then_inc(pool_step, 1)
                    nc.vector.scalar_tensor_tensor(high, high, vec[64:P, V_SO:V_SO + 1],
                                                   joints(buf, 64, P, 1, u0, us), ALU.mult, ALU.add)
                if part != 0:
                    dve.wait_ge(pool_step, m * 2 * NK + 2 * k + 1)
                    nc.vector.tensor_tensor(low, low, mf[:, 0:us, 2:T + 2], ALU.max).then_inc(pool_step, 1)
                    dve.wait_ge(pool_step, m * 2 * NK + 2 * k + 2)
                    nc.vector.scalar_tensor_tensor(low, low, vec[0:64, V_SO:V_SO + 1], joints(buf, 0, 64, 1, u0, us),
                                                   ALU.mult, ALU.add).then_inc(sumB_ready, 1)

            def convolved(m, k, buf):
                u0, us = UCH[k]
                w = us * T
                dve.wait_ge(conv_full, m * NK + k + 1)
                if some(m * NK + k):
                    dve.wait_ge(outA_done, m * NK + k)
                nc.vector.tensor_tensor(sumA[0:64, 0:w].rearrange("c (u t) -> c u t", t=T),
                                        ps_h[0:64, 0:w].rearrange("c (u t) -> c u t", t=T),
                                        joints(buf, 0, 64, 0, u0, us), ALU.add)
                nc.vector.tensor_tensor(
                    sumA[64:P, 0:w].rearrange("c (u q s) -> c u s q", s=2, u=us),
                    ps_h[64:P, 0:w].rearrange("c (u s q) -> c u s q", s=2, u=us),
                    joints(buf, 64, P, 0, u0, us).rearrange("c u (q s) -> c u s q", s=2),
                    ALU.add).then_inc(sumA_ready, 1)

            def step(n, h, r, head, tail, ahead):
                m = n - 1
                buf = xb[(r - 1) % NX]
                h1, r1 = following(h, r)
                for k in range(3):
                    if tail and k == 2:
                        convolved(m, 0, buf)
                    if head:
                        take_tr(n, k)
                    if tail and k:
                        h_high(m, k - 1)
                        pooled(m, k - 1, buf)
                    if tail:
                        both_added(m, k, buf)
                        both_low(m, k)
                if head:
                    take_tr(n, 3, (0,))
                if tail:
                    convolved(m, 1, buf)
                if head:
                    take_tr(n, 3, range(1, 5))
                if tail:
                    h_high(m, 2)
                if head:
                    take_tr(n, 3, (5, 6))
                if tail:
                    both_added(m, 3, buf)
                if head:
                    take_tr(n, 4, (0, 1))
                if tail:
                    both_low(m, 3)
                if head:
                    take_tr(n, 4, (2, 3))
                if tail:
                    pooled(m, 2, buf)
                    convolved(m, 2, buf)
                if head:
                    take_top(n, 1)
                    take_top(n, 3)
                if tail:
                    both_added(m, 4, buf)
                if head:
                    take_top(n, 5)
                if tail:
                    pooled(m, 3, buf, 0)
                if head:
                    take_top(n, 7)
                if tail:
                    h_high(m, 3)
                    both_low(m, 4)
                    pooled(m, 3, buf, 1)
                    convolved(m, 3, buf)
                    h_high(m, 4)
                    pooled(m, 4, buf)
                    convolved(m, 4, buf)
                if ahead:
                    mean(n + 1, h1, r1)
                    differences(n + 1)

            mean(0, 0, 0)
            differences(0)
            all_samples(dve, step)

        @block.tensor
        def _(pe):
            def three(out, w, a, first, last):
                nc.tensor.matmul(out, w[0], a[0], start=first, stop=False)
                nc.tensor.matmul(out, w[0], a[1], start=False, stop=False)
                return nc.tensor.matmul(out, w[1], a[0], start=False, stop=last)

            def s1_half(n, k, b, kb):
                w = HCH[k][1] * V
                if b == 0 and kb == 0:
                    pe.wait_ge(xl_ready, n * NK + k + 1)
                before = n * 3 * NK + 3 * k + b // 2
                if kb == 0 and some(before):
                    pe.wait_ge(inp_taken[b % 2], before)
                cols = slice(b * P, (b + 1) * P)
                ins = three(ps_inp[b % 2][:, 0:w], (rwh[:, kb, cols], rwl[:, kb, cols]),
                            (xh[k % 2][:, kb, 0:w], xl[k % 2][:, kb, 0:w]), kb == 0, kb == CB - 1)
                if kb == CB - 1:
                    ins.then_inc(inp_full[b % 2], 1)

            def s1(n, k, b):
                for kb in range(CB):
                    s1_half(n, k, b, kb)

            def tr1(n, k, j):
                g = TR_OF[k] + j
                if j == 0:
                    for b in range(2):
                        pe.wait_ge(inp_taken[b], n * 3 * NK + 3 * (k + 1))
                pe.wait_ge(tr_taken[g % 2], n * TRB + g // 2)
                for t in range(4):
                    ins = nc.tensor.transpose(ps_tr[g % 2][0:KP, t * P:(t + 1) * P], inp[k % 2][:, 4 * j + t, :],
                                              ident[:, :])
                ins.then_inc(tr_full[g % 2], 1)

            def projections(n):
                pe.wait_ge(xm_ready, n + 1)
                for s in range(2):
                    g = G_PROJ + s
                    if some(n * TRB):
                        pe.wait_ge(tr_taken[g % 2], n * TRB)
                    for kb in range(CB):
                        ins = nc.tensor.matmul(ps_tr[g % 2][0:SUB * REL, 0:V],
                                               c12T[:, kb, s * SUB * REL:(s + 1) * SUB * REL], xm[:, kb, :],
                                               start=kb == 0, stop=kb == CB - 1)
                    ins.then_inc(tr_full[g % 2], 1)

            def topologies(n, j):
                g = G_TOP + j
                if j == 0:
                    pe.wait_ge(tanh_ready, n + 1)
                pe.wait_ge(tr_taken[g % 2], n * TRB + g // 2)
                for uu in range(min(UPG, V - j * UPG)):
                    u = j * UPG + uu
                    for c in range(2):
                        w0 = u * MW + (KA if c == 0 else 0)
                        ins = nc.tensor.matmul(ps_tr[g % 2][0:KP, (2 * uu + c) * P:(2 * uu + c + 1) * P],
                                               mbd[:, w0:w0 + KP], c3T[:, c * P:(c + 1) * P],
                                               start=True, stop=True)
                ins.then_inc(tr_full[g % 2], 1)

            def s2(n, j):
                g = G_S2 + j
                if j == 0:
                    for b in range(2):
                        pe.wait_ge(tr_taken[b], n * TRB + groups_before(G_S2, b))
                else:
                    pe.wait_ge(tr_taken[g % 2], n * TRB + g // 2)
                for i in range(min(PPG, P - j * PPG)):
                    p = j * PPG + i
                    ins = nc.tensor.matmul(ps_tr[g % 2][:, i * SW:(i + 1) * SW], inpT[0:KP, p, :],
                                           top[0:KP, p * 2 * V:p * 2 * V + SW], start=True, stop=True)
                ins.then_inc(tr_full[g % 2], 1)

            def tr2(m, k):
                u0, us = UCH[k]
                if k == 0:
                    for b in range(2):
                        pe.wait_ge(tr_taken[b], m * TRB + TRB)
                for cb in range(CB):
                    if some(m * NK + k):
                        pe.wait_ge(y_split[cb], m * NK + k)
                    for j in range(us):
                        src = top[:, 0:P * 2 * V].rearrange("t (p c u) -> t c u p", c=2, u=V)[:, cb, u0 + j, :]
                        ins = nc.tensor.transpose(ps_y[cb][:, j * T:(j + 1) * T], src, ident[:, :])
                    ins.then_inc(y_full[cb], 1)

            def s3_half(m, k, blk, kb):
                w = UCH[k][1] * T
                if blk and kb == 0:
                    for cb in range(CB):
                        pe.wait_ge(y_split[cb], m * NK + k + 1)
                if kb == 0 and some(m * NK + k):
                    pe.wait_ge(outB_done if blk else sumA_ready, m * NK + k)
                cols = slice(blk * P, (blk + 1) * P)
                ins = three((ps_m if blk else ps_h)[:, 0:w], (w3h[:, kb, cols], w3l[:, kb, cols]),
                            (yh[:, kb, 0:w], yl[:, kb, 0:w]), kb == 0, kb == CB - 1)
                if kb == CB - 1:
                    ins.then_inc(m_full if blk else h_full, 1)

            S3 = ((1, 0), (1, 1), (0, 0), (0, 1))

            def conv(m, k, taps=range(KS)):
                us = UCH[k][1]
                if 0 in taps:
                    pe.wait_ge(hl_ready, m * NK + k + 1)
                for tap in taps:
                    def at(h):
                        return h[:, 0:us, :].rearrange("c u (s q) -> c u s q", s=2)[:, :, :, tap:tap + T // 2]
                    ins = three(ps_h[:, 0:us * T], (w2h[:, tap, :], w2l[:, tap, :]), (at(hh), at(hl)),
                                tap == 0, tap == KS - 1)
                if KS - 1 in taps:
                    ins.then_inc(conv_full, 1)

            def step(n, h, r, head, tail, ahead):
                m = n - 1
                if head:
                    tr1(n, 0, 0)
                    for j, (k, b, kb) in enumerate(((1, 5, 0), (1, 5, 1), (2, 0, 0), (2, 0, 1), (2, 1, 0))):
                        s1_half(n, k, b, kb)
                        tr1(n, 0, j + 1)
                    tr1(n, 0, 6)
                    s1_half(n, 2, 1, 1)
                if tail:
                    tr2(m, 0)
                if head:
                    for b in range(2, BLK):
                        s1(n, 2, b)
                for k in range(1, 3):
                    if head:
                        tr1(n, k, 0)
                        s1_half(n, k + 2, 0, 0)
                        tr1(n, k, 1)
                    for j, half in enumerate(S3):
                        if tail:
                            s3_half(m, k - 1, *half)
                        if head:
                            tr1(n, k, j + 2)
                    if head:
                        tr1(n, k, 6)
                        s1_half(n, k + 2, 0, 1)
                        s1(n, k + 2, 1)
                    if tail:
                        tr2(m, k)
                    if head:
                        s1(n, k + 2, 2)
                        s1(n, k + 2, 3)
                        if k == 1:
                            s1(n, 3, 4)
                            s1(n, 3, 5)
                    if tail:
                        conv(m, k - 1)
                if head:
                    tr1(n, 3, 0)
                    tr1(n, 3, 1)
                for j, half in enumerate(S3):
                    if tail:
                        s3_half(m, 2, *half)
                    if head:
                        tr1(n, 3, j + 2)
                if head:
                    s1(n, 4, 4)
                    tr1(n, 3, 6)
                    s1(n, 4, 5)
                if tail:
                    tr2(m, 3)
                if head:
                    tr1(n, 4, 0)
                    tr1(n, 4, 1)
                if tail:
                    conv(m, 2, (0,))
                if head:
                    tr1(n, 4, 2)
                if tail:
                    conv(m, 2, (1,))
                if head:
                    tr1(n, 4, 3)
                if tail:
                    conv(m, 2, (2, 3, 4))
                    tr2(m, 4)
                for j in range(N_TOP):
                    if head:
                        topologies(n, j)
                    if ahead and j in (1, N_TOP - 1):
                        s1(n + 1, 0, 0 if j == 1 else 1)
                    if tail and 3 <= j < 3 + len(S3):
                        s3_half(m, 3, *S3[j - 3])
                for j in range(N_S2):
                    if head:
                        s2(n, j)
                    if ahead:
                        for b in ahead_blocks(j):
                            s1(n + 1, b // BLK, b % BLK)
                    if tail and j == 2:
                        conv(m, 3)
                    if tail and j == 4:
                        for half in S3[:2]:
                            s3_half(m, 4, *half)
                    if tail and j == 6:
                        for half in S3[2:]:
                            s3_half(m, 4, *half)
                    if tail and j == 9:
                        conv(m, 4)
                if ahead:
                    projections(n + 1)
                    s1(n + 1, 1, 4)

            pe.wait_ge(setup_done, 1)
            for b in range(AHEAD_S2):
                s1(0, b // BLK, b % BLK)
            projections(0)
            s1(0, 1, 4)
            all_samples(pe, step)


def kernel(**a):
    import numpy as np
    import concourse.bacc as bacc
    from concourse.bass_utils import run_bass_kernel_spmd

    a = {k.replace("L0_conv_", ""): np.asarray(v) for k, v in a.items()}
    N, C = a["x"].shape[:2]
    f = np.float32
    z64 = np.zeros(64, f)

    def kblocks(w):
        return np.ascontiguousarray(w.reshape(CB, P, -1).transpose(1, 0, 2).reshape(P, -1))

    rw = a["g_rw"].reshape(SUB, CB, P, C).transpose(3, 1, 0, 2).reshape(C, BLK * P)
    w3 = np.concatenate([a["br_w1"].reshape(2 * 64, C), a["mp_w1"], a["p_w"]], 0).T
    w2 = np.zeros((P, KS, P), f)
    for k in range(2):
        w2[64 * k:64 * k + 64, :, 64 * k:64 * k + 64] = a["br_w2"][k].transpose(1, 2, 0)
    c12 = np.concatenate([a["g_c1w"].reshape(SUB * REL, C), a["g_c2w"].reshape(SUB * REL, C)], 0).T
    c3 = np.concatenate([a["g_c3w"].transpose(0, 2, 1).reshape(SUB * REL, C), a["g_c3b"], np.ones((1, C), f)], 0)
    atop = np.ascontiguousarray(a["A"].transpose(1, 0, 2)).reshape(1, V, KA)
    ind = np.ascontiguousarray(np.broadcast_to(np.repeat(np.eye(SUB, dtype=f), V, 1)[:, None, :], (SUB, V, KA)))
    vecs = np.zeros((P, NV), f)
    vecs[:, V_GS:V_GS + 2] = a["gbn_s"].reshape(CB, P).T
    vecs[:, V_GB:V_GB + 2] = a["gbn_b"].reshape(CB, P).T
    vecs[:, V_RB:V_RB + 6] = a["g_rb"].reshape(SUB, CB, P).transpose(2, 1, 0).reshape(P, BLK)
    for col, v in ((V_S1, a["br_s1"].reshape(P)), (V_B1, a["br_b1"].reshape(P)), (V_BB1, a["br_bb1"].reshape(P)),
                   (V_S2, a["br_s2"].reshape(P)), (V_B2, a["br_b2"].reshape(P)), (V_BB2, a["br_bb2"].reshape(P)),
                   (V_SM, np.concatenate([a["mp_s1"], z64])), (V_BM, np.concatenate([a["mp_b1"], z64])),
                   (V_BBM, np.concatenate([a["mp_bb1"], z64])), (V_SO, np.concatenate([a["mp_s2"], a["p_s"]])),
                   (V_BO, np.concatenate([z64, a["p_b"]])), (V_BBO, np.concatenate([a["mp_bb2"], a["p_bb"]]))):
        vecs[:, col] = v
    vecs[0:SUB * REL, V_C1] = a["g_c1b"].reshape(-1)
    vecs[0:SUB * REL, V_C2] = a["g_c2b"].reshape(-1)
    vecs[:, V_AL] = a["alpha"][0]
    arrays = {
        "x": np.ascontiguousarray(a["x"].reshape(N, C, TV)), "rw": kblocks(rw), "c12": kblocks(c12), "c3": c3,
        "atop": atop, "ind": ind, "w3": kblocks(w3), "w2": w2.reshape(P, KS * P),
        "s2row": np.ascontiguousarray(a["br_s2"].reshape(P)), "ident": np.eye(P, dtype=f), "vecs": vecs,
    }
    nc = bacc.Bacc("TRN2", target_bir_lowering=False, num_devices=1,
                   dynamic_dma_scratch_size=1024)
    args, ins = [], {}
    for name, arr in arrays.items():
        arr = np.ascontiguousarray(arr)
        ins[f"in_{name}"] = arr
        args.append(nc.dram_tensor(f"in_{name}", arr.shape, mybir.dt.from_np(arr.dtype), kind="ExternalInput").ap())
    args.append(nc.dram_tensor("out", (N, C, TV), F32, kind="ExternalOutput").ap())
    args[2] = args[2].rearrange("p (k o) -> p k o", k=CB)
    build(nc, *args)
    r = run_bass_kernel_spmd(nc, [ins], core_ids=[0])
    return r.results[0]["out"].reshape(N, C, T, V)
```

```python
from contextlib import ExitStack

import concourse.bass as bass
from concourse import mybir

F32 = mybir.dt.float32
F32R = mybir.dt.float32r
ALU = mybir.AluOpType
ACT = mybir.ActivationFunctionType
AX = mybir.AxisListType

P = 128
T = 128
V = 17
TV = T * V
CB = 2
SUB = 3
REL = 32
KS = 5
BLK = SUB * CB
KA = SUB * V
KP = 2 * KA
KM = SUB * REL + SUB + 1
MW = 2 * KA

TCH = 28
HCH = [(t0, min(TCH, T - t0)) for t0 in range(0, T, TCH)]
NK = len(HCH)
UCH = [(-(-k * V // NK), -(-(k + 1) * V // NK) - -(-k * V // NK)) for k in range(NK)]
assert NK == len(UCH) == 5
XW = TCH * V

BR = 2
CH = 64
SHIFTS = 3
Q = (T // 2, T // 4)
RUN = (Q[0] + 2, Q[1] + 2)
LH = RUN[0] + 2 * RUN[1]
BRW = 4 * Q[0]

G_PROJ = 0
TR_OF = [2 + t0 // 4 for t0, _ in HCH]
G_TOP = 2 + T // 4
UPG = 2
N_TOP = -(-V // UPG)
G_S2 = G_TOP + N_TOP
SW = 4 * V
PPG = 512 // SW
N_S2 = -(-P // PPG)
G_END = G_S2 + N_S2
assert G_END % 2 == 0
TRB = G_END // 2


def some(count):
    return not isinstance(count, int) or count > 0


def groups_before(g, bank):
    return (g + 1 - bank) // 2


AHEAD = 2
AHEAD_TOP = 4
AHEAD_S2 = AHEAD * BLK - 2


def ahead_blocks(j):
    def until(x):
        return AHEAD_TOP + x * (AHEAD_S2 - AHEAD_TOP) // (N_S2 - 1)
    return range(until(j - 1), until(j)) if j else range(0)


V_GS, V_GB, V_RB, V_S1, V_B1, V_BB1, V_B2, V_BB2 = 0, 2, 4, 10, 11, 12, 13, 14
V_SM, V_BM, V_BBM, V_SO, V_BO, V_BBO, V_C1, V_C2, V_AL, V_S2 = 15, 16, 17, 18, 19, 20, 21, 22, 23, 24
NV = 25
D_IN, D_H, D_A, D_M, D_B, D_D = 0, 6, 7, 8, 9, 10
ND = 11


def build(nc, x, rw, c12, c3, atop, ind, w3, w2, s2row, ident_in, vecs_in, out):
    NS = x.shape[0]
    NX = 3
    assert NS % NX == 0 and NS >= 2 * NX
    ctx = ExitStack()
    with ctx:
        def sb(name, shape, dt=F32):
            return ctx.enter_context(nc.sbuf_tensor(name, shape, dt))

        def sem(name):
            return ctx.enter_context(nc.semaphore(name))

        xb = [sb(f"x{i}", [P, CB, TV]) for i in range(NX)]
        xh = [sb(f"x_high{i}", [P, CB, XW], F32R) for i in range(2)]
        xl = [sb(f"x_low{i}", [P, CB, XW], F32R) for i in range(2)]
        inp = [sb(f"inp{i}", [P, TCH, KP]) for i in range(2)]
        inpT = sb("inpT", [P, P, T])
        top = sb("top", [P, (P + 1) * 2 * V])
        yh = sb("y_high", [P, CB, 512], F32R)
        yl = sb("y_low", [P, CB, 512], F32R)
        hf = sb("h", [P, 4, LH])
        hh = sb("h_high", [P, 4, LH], F32R)
        hl = sb("h_low", [P, 4, LH], F32R)
        mf = sb("pool_in", [CH, 4, T + 2])
        sumA = sb("sumA", [P, 512])
        rwh = sb("rw_high", [P, CB, BLK * P], F32R)
        rwl = sb("rw_low", [P, CB, BLK * P], F32R)
        w3h = sb("w3_high", [P, CB, 2 * P], F32R)
        w3l = sb("w3_low", [P, CB, 2 * P], F32R)
        w2h = sb("w2_high", [P, BR * SHIFTS, P], F32R)
        w2l = sb("w2_low", [P, BR * SHIFTS, P], F32R)
        mbd = sb("tanh_blocks", [KM, KA + V * MW])
        c3T = sb("c3T", [KM, CB * P])
        c12T = sb("c12T", [P, CB, 2 * SUB * REL])
        ident = sb("ident", [P, P])
        vec = sb("vec", [P, NV])
        der = sb("derived", [P, ND])
        xm = sb("xm", [P, CB, V])
        proj2 = sb("proj2", [SUB * REL, V])
        diff = sb("diff", [SUB * REL, V * V])

        ps_inp = [ctx.enter_context(nc.psum_tensor(f"ps_inp{i}", [P, 512], F32)) for i in range(2)]
        ps_tr = [ctx.enter_context(nc.psum_tensor(f"ps_tr{i}", [P, 512], F32)) for i in range(2)]
        ps_y = [ctx.enter_context(nc.psum_tensor(f"ps_y{i}", [P, 512], F32)) for i in range(2)]
        ps_h = ctx.enter_context(nc.psum_tensor("ps_h", [P, 512], F32))
        ps_m = ctx.enter_context(nc.psum_tensor("ps_m", [P, 512], F32))

        stage = inpT[:, :, :].rearrange("p a b -> p (a b)")
        st_rw = stage[:, 0:CB * BLK * P]
        st_w3 = stage[:, 2048:2048 + CB * 2 * P]
        st_w2 = stage[:, 3072:3072 + BR * SHIFTS * P]
        st_s2 = stage[:, 4096:4096 + P]

        rw_loaded = sem("rw_loaded")
        consts_loaded = sem("consts_loaded")
        blocks_cleared = sem("blocks_cleared")
        rows_loaded = sem("rows_loaded")
        setup_step = sem("setup_step")
        rw_split = sem("rw_split")
        setup_done = sem("setup_done")
        x_loaded = [sem(f"x_loaded{i}") for i in range(NX)]
        out_stored = [sem(f"out_stored{i}") for i in range(NX)]
        xh_ready = sem("xh_ready")
        xl_ready = sem("xl_ready")
        inp_full = [sem(f"inp_full{i}") for i in range(2)]
        inp_taken = [sem(f"inp_taken{i}") for i in range(2)]
        tr_full = [sem(f"tr_full{i}") for i in range(2)]
        tr_taken = [sem(f"tr_taken{i}") for i in range(2)]
        xm_ready = sem("xm_ready")
        tanh_ready = sem("tanh_ready")
        y_full = [sem(f"y_full{i}") for i in range(2)]
        y_added = [sem(f"y_added{i}") for i in range(2)]
        yh_ready = [sem(f"yh_ready{i}") for i in range(2)]
        y_split = [sem(f"y_split{i}") for i in range(2)]
        h_full = sem("h_full")
        m_full = sem("m_full")
        hf_ready = sem("hf_ready")
        mf_ready = sem("mf_ready")
        hh_ready = sem("hh_ready")
        hl_ready = sem("hl_ready")
        conv_full = sem("conv_full")
        pool_step = sem("pool_step")
        sumA_ready = sem("sumA_ready")
        sumB_ready = sem("sumB_ready")
        outA_done = sem("outA_done")
        outB_done = sem("outB_done")
        block = ctx.enter_context(nc.Block())

        def all_samples(eng, step):
            step(0, 0, 0, True, False, True)
            step(1, 0, 1, True, True, True)
            with eng.Fori(0, NS // NX - 1) as i:
                step(i * NX + 2, i, 2, True, True, True)
                step(i * NX + 3, i + 1, 0, True, True, True)
                step(i * NX + 4, i + 1, 1, True, True, True)
            step(NS - 1, NS // NX - 1, 2, True, True, False)
            step(NS, NS // NX, 0, False, True, False)

        def joints(buf, lo, hi, cb, u0, us):
            return buf[lo:hi, cb, :].rearrange("c (t v) -> c v t", v=V)[:, u0:u0 + us, :]

        def runs(h, br, at):
            if br == 0:
                return h[:, :, at:at + Q[0]]
            return h[:, :, RUN[0]:LH].rearrange("c u (s q) -> c u s q", s=2)[:, :, :, at:at + Q[1]]

        def steps_of(cols, br, pair):
            if br == 0:
                return cols.rearrange("c (u q e) -> c e u q", e=2, q=Q[0])[:, pair]
            return cols.rearrange("c (u q e s) -> c e u s q", e=2, s=2, q=Q[1])[:, pair]

        def following(h, r):
            return (h + 1, 0) if r == NX - 1 else (h, r + 1)

        @block.sync
        def _(sp):
            def load(n, r):
                for cb in range(CB):
                    sp.dma_start(xb[r][:, cb, :], x[n, cb * P:(cb + 1) * P, :]).then_inc(x_loaded[r], 16)

            def finish(n, h, r, again):
                sp.wait_ge(outA_done, n * NK + NK)
                sp.wait_ge(outB_done, n * NK + NK)
                for cb in range(CB):
                    sp.dma_start(out[n, cb * P:(cb + 1) * P, :], xb[r][:, cb, :]).then_inc(out_stored[r], 16)
                sp.wait_ge(out_stored[r], h * 32 + 32)
                if again:
                    load(n + NX, r)

            sp.dma_start(st_rw, rw).then_inc(rw_loaded, 16)
            sp.dma_start(vec[:, :], vecs_in).then_inc(rw_loaded, 16)
            load(0, 0)
            sp.dma_start(c12T[:, :, :], c12).then_inc(consts_loaded, 16)
            sp.dma_start(ident[:, :], ident_in).then_inc(consts_loaded, 16)
            sp.dma_start(c3T[:, :], c3).then_inc(consts_loaded, 16)
            sp.dma_start(st_w3, w3).then_inc(consts_loaded, 16)
            sp.dma_start(st_w2, w2).then_inc(consts_loaded, 16)
            sp.dma_start(st_s2, s2row.partition_broadcast(P)).then_inc(consts_loaded, 16)
            sp.wait_ge(blocks_cleared, 1)
            for lo, hi, src in ((SUB * REL, KM - 1, ind), (KM - 1, KM, atop)):
                rows = mbd[lo:hi, :]
                dst = bass.AP(mbd, rows.offset + KA, [rows.ap[0], [MW, V], [1, KA]])
                sp.dma_start(dst, src).then_inc(rows_loaded, 16)
            load(1, 1)
            load(2, 2)
            with sp.Fori(0, NS // NX - 1) as i:
                for r in range(NX):
                    finish(i * NX + r, i, r, True)
            for r in range(NX):
                finish(NS - NX + r, NS // NX - 1, r, False)

        @block.gpsimd
        def _(pool):
            def x_low(n, r, k):
                t0, ts = HCH[k]
                pool.wait_ge(xh_ready, n * NK + k + 1)
                nc.gpsimd.tensor_tensor(xl[k % 2][:, :, 0:ts * V], xb[r][:, :, t0 * V:(t0 + ts) * V],
                                        xh[k % 2][:, :, 0:ts * V].bitcast(F32), ALU.subtract).then_inc(xl_ready, 1)

            def h_low(m, k):
                us = UCH[k][1]
                pool.wait_ge(hh_ready, m * NK + k + 1)
                nc.gpsimd.tensor_tensor(hl[:, 0:us, :], hf[:, 0:us, :], hh[:, 0:us, :].bitcast(F32),
                                        ALU.subtract).then_inc(hl_ready, 1)

            def step(n, h, r, head, tail, ahead):
                h1, r1 = following(h, r)
                if head:
                    x_low(n, r, 3)
                    x_low(n, r, 4)
                if tail:
                    h_low(n - 1, 0)
                    h_low(n - 1, 1)
                if ahead:
                    x_low(n + 1, r1, 0)
                if tail:
                    h_low(n - 1, 2)
                if ahead:
                    x_low(n + 1, r1, 1)
                for k in range(3, NK):
                    if tail:
                        h_low(n - 1, k)
                if ahead:
                    x_low(n + 1, r1, 2)

            for k in range(3):
                x_low(0, 0, k)
            all_samples(pool, step)

        @block.scalar
        def _(act):
            def x_high(n, h, r, k):
                t0, ts = HCH[k]
                if k == 0:
                    act.wait_ge(x_loaded[r], h * 32 + 32)
                nc.scalar.activation(xh[k % 2][:, :, 0:ts * V], xb[r][:, :, t0 * V:(t0 + ts) * V],
                                     ACT.Copy).then_inc(xh_ready, 1)

            def take_inp(n, k, b):
                ts = HCH[k][1]
                cb = b // SUB
                act.wait_ge(inp_full[b % 2], n * 3 * NK + 3 * k + b // 2 + 1)
                nc.scalar.activation(inp[k % 2][:, 0:ts, b * V:(b + 1) * V],
                                     ps_inp[b % 2][:, 0:ts * V].rearrange("c (t v) -> c t v", v=V), ACT.Identity,
                                     bias=der[:, D_IN + b:D_IN + b + 1],
                                     scale=vec[:, V_GS + cb:V_GS + cb + 1]).then_inc(inp_taken[b % 2], 1)

            def take_tr(n, k, j):
                t0 = HCH[k][0] + 4 * j
                g = TR_OF[k] + j
                if g % 2 == 0:
                    act.wait_ge(tr_full[0], n * TRB + g // 2 + 1)
                    nc.scalar.activation(inpT[0:KP, :, t0:t0 + 4], ps_tr[0][0:KP, :].rearrange("k (t p) -> k p t", t=4),
                                         ACT.Copy).then_inc(tr_taken[0], 1)

            def take_top(n, j):
                g = G_TOP + j
                us = min(UPG, V - j * UPG)
                act.wait_ge(tr_full[g % 2], n * TRB + g // 2 + 1)
                nc.scalar.activation(
                    top[0:KP, 0:P * 2 * V].rearrange("k (p c u) -> k u c p", c=2, u=V)[:, j * UPG:j * UPG + us],
                    ps_tr[g % 2][0:KP, 0:us * 2 * P].rearrange("k (u c p) -> k u c p", c=2, u=us), ACT.Copy
                ).then_inc(tr_taken[g % 2], 1)

            def tanh(n):
                act.wait_ge(tr_taken[0], n * TRB + G_PROJ // 2 + 1)
                for i in range(SUB):
                    rows = mbd[REL * i:REL * (i + 1), :]
                    dst = bass.AP(mbd, rows.offset + KA + V * i, [rows.ap[0], [MW, V], [1, V]])
                    ins = nc.scalar.activation(dst, diff[REL * i:REL * (i + 1), :].rearrange("r (u v) -> r u v", v=V),
                                               ACT.Tanh, bias=der[REL * i:REL * (i + 1), D_D:D_D + 1], scale=1.0 / T)
                ins.then_inc(tanh_ready, 1)

            def y_high(m, k, cb):
                w = UCH[k][1] * T
                act.wait_ge(y_added[cb], m * NK + k + 1)
                nc.scalar.activation(yh[:, cb, 0:w], ps_y[cb][:, 0:w], ACT.Relu).then_inc(yh_ready[cb], 1)

            def hidden_m(m, k):
                us = UCH[k][1]
                act.wait_ge(m_full, m * NK + k + 1)
                nc.scalar.activation(mf[:, 0:us, 1:T + 1], ps_m[0:CH, 0:us * T].rearrange("c (u t) -> c u t", t=T),
                                     ACT.Relu, bias=der[0:CH, D_M:D_M + 1],
                                     scale=vec[0:CH, V_SM:V_SM + 1]).then_inc(mf_ready, 1)

            def hidden_h(m, k):
                us = UCH[k][1]
                act.wait_ge(h_full, m * NK + k + 1)
                for br in range(BR):
                    rows = slice(br * CH, (br + 1) * CH)
                    for pair in range(2):
                        dst = runs(hf[pair * CH:(pair + 1) * CH, 0:us, :], br, 1)
                        ins = nc.scalar.activation(dst, steps_of(ps_h[rows, 0:us * T], br, pair), ACT.Relu,
                                                   bias=der[rows, D_H:D_H + 1], scale=vec[rows, V_S1:V_S1 + 1])
                ins.then_inc(hf_ready, 1)

            def outA(m, k, buf):
                u0, us = UCH[k]
                act.wait_ge(sumA_ready, m * NK + k + 1)
                nc.scalar.activation(joints(buf, 0, P, 0, u0, us),
                                     sumA[:, 0:us * T].rearrange("c (u t) -> c u t", t=T), ACT.Relu,
                                     bias=der[:, D_A:D_A + 1]).then_inc(outA_done, 1)

            def outB(m, k, buf):
                u0, us = UCH[k]
                act.wait_ge(sumB_ready, m * NK + k + 1)
                nc.scalar.activation(joints(buf, 0, P, 1, u0, us),
                                     ps_m[:, 0:us * T].rearrange("c (u t) -> c u t", t=T), ACT.Relu,
                                     bias=der[:, D_B:D_B + 1]).then_inc(outB_done, 1)

            def take_s2(n, j):
                g = G_S2 + j
                pairs = min(PPG, P - j * PPG)
                c0 = j * PPG * 2 * V
                act.wait_ge(tr_full[g % 2], n * TRB + g // 2 + 1)
                nc.scalar.activation(top[:, c0:c0 + pairs * 2 * V].rearrange("t (i w) -> t i w", w=2 * V),
                                     ps_tr[g % 2][:, 0:pairs * SW].rearrange("t (i w) -> t i w", w=SW)[:, :, 0:2 * V],
                                     ACT.Copy).then_inc(tr_taken[g % 2], 1)

            def step(n, h, r, head, tail, ahead):
                m = n - 1
                buf = xb[(r - 1) % NX]
                h1, r1 = following(h, r)
                if head:
                    take_tr(n, 0, 0)
                    take_inp(n, 1, BLK - 1)
                    take_tr(n, 0, 2)
                    x_high(n, h, r, 3)
                    take_tr(n, 0, 4)
                    take_tr(n, 0, 6)
                    for b in range(3):
                        take_inp(n, 2, b)
                if tail:
                    y_high(m, 0, 0)
                if head:
                    take_inp(n, 2, 3)
                if tail:
                    y_high(m, 0, 1)
                if head:
                    take_inp(n, 2, 4)
                    take_inp(n, 2, 5)
                    x_high(n, h, r, 4)
                for k in range(1, 3):
                    if head:
                        for j in range(2):
                            take_tr(n, k, j)
                    if tail and k == 2:
                        outA(m, 0, buf)
                    if head:
                        take_tr(n, k, 2)
                        take_tr(n, k, 3)
                    if tail:
                        hidden_h(m, k - 1)
                    if head:
                        take_tr(n, k, 4)
                    if tail:
                        hidden_m(m, k - 1)
                    if head:
                        take_tr(n, k, 5)
                        take_tr(n, k, 6)
                        if k == 1:
                            act.wait_ge(tr_full[1], n * TRB + (TR_OF[1] + 6) // 2 + 1)
                        for b in range(3):
                            take_inp(n, k + 2, b)
                    if tail:
                        y_high(m, k, 0)
                    if head:
                        take_inp(n, k + 2, 3)
                    if tail:
                        y_high(m, k, 1)
                    if head and k == 1:
                        tanh(n)
                    if tail:
                        outB(m, k - 1, buf)
                    if head:
                        take_inp(n, k + 2, 4)
                        take_inp(n, k + 2, 5)
                if head:
                    take_tr(n, 3, 1)
                if ahead:
                    x_high(n + 1, h1, r1, 0)
                if head:
                    take_tr(n, 3, 3)
                if tail:
                    hidden_h(m, 2)
                if head:
                    take_tr(n, 3, 5)
                if tail:
                    hidden_m(m, 2)
                    outA(m, 1, buf)
                if head:
                    take_tr(n, 4, 0)
                if tail:
                    y_high(m, 3, 0)
                    y_high(m, 3, 1)
                if head:
                    take_tr(n, 4, 2)
                if ahead:
                    act.wait_ge(tr_full[1], n * TRB + (TR_OF[4] + 3) // 2 + 1)
                    take_inp(n + 1, 0, 0)
                    take_inp(n + 1, 0, 1)
                if head:
                    take_top(n, 0)
                if ahead:
                    x_high(n + 1, h1, r1, 1)
                    take_inp(n + 1, 0, 2)
                if tail:
                    outB(m, 2, buf)
                if head:
                    take_top(n, 2)
                if tail:
                    outA(m, 2, buf)
                if head:
                    take_top(n, 4)
                if tail:
                    hidden_h(m, 3)
                if head:
                    take_top(n, 6)
                if tail:
                    hidden_m(m, 3)
                if head:
                    take_top(n, 8)
                if tail:
                    y_high(m, 4, 0)
                    y_high(m, 4, 1)
                if ahead:
                    take_inp(n + 1, 0, 3)
                for j in range(N_S2):
                    if head:
                        take_s2(n, j)
                    if ahead:
                        for b in ahead_blocks(j):
                            take_inp(n + 1, b // BLK, b % BLK)
                            if b == BLK - 1:
                                x_high(n + 1, h1, r1, 2)
                    if tail and j == 1:
                        outB(m, 3, buf)
                    if tail and j == 4:
                        outA(m, 3, buf)
                    if tail and j == 5:
                        hidden_h(m, 4)
                    if tail and j == 7:
                        hidden_m(m, 4)
                    if tail and j == 9:
                        outB(m, 4, buf)
                    if tail and j == 11:
                        outA(m, 4, buf)
                if ahead:
                    take_inp(n + 1, 1, 4)

            x_high(0, 0, 0, 0)
            x_high(0, 0, 0, 1)
            act.wait_ge(rw_split, 1)
            for b in range(AHEAD * BLK - 1):
                take_inp(0, b // BLK, b % BLK)
                if b == BLK - 1:
                    x_high(0, 0, 0, 2)
            act.wait_ge(setup_done, 1)
            all_samples(act, step)

        @block.vector
        def _(dve):
            steps = [0]

            def then(ins):
                steps[0] += 1
                ins.then_inc(setup_step, 1)
                dve.wait_ge(setup_step, steps[0])

            nc.vector.memset(mbd[:, :], 0.0).then_inc(blocks_cleared, 1)
            nc.vector.memset(hf[:, :, :], 0.0)
            nc.vector.memset(top[:, P * 2 * V:], 0.0)
            nc.vector.memset(mf[:, :, :], 0.0)
            def high_low(h, l, src):
                then(nc.vector.tensor_copy(h, src))
                nc.vector.tensor_tensor(l, src, h.bitcast(F32), ALU.subtract)

            dve.wait_ge(rw_loaded, 32)
            for cb in range(CB):
                nc.vector.tensor_scalar(der[:, D_IN + SUB * cb:D_IN + SUB * cb + SUB],
                                        vec[:, V_RB + SUB * cb:V_RB + SUB * cb + SUB],
                                        vec[:, V_GS + cb:V_GS + cb + 1], None, ALU.mult)
            then(nc.vector.tensor_copy(rwh[:, :, :].rearrange("p a b -> p (a b)"), st_rw))
            nc.vector.tensor_tensor(rwl[:, :, :].rearrange("p a b -> p (a b)"), st_rw,
                                    rwh[:, :, :].rearrange("p a b -> p (a b)").bitcast(F32),
                                    ALU.subtract).then_inc(rw_split, 1)
            dve.wait_ge(consts_loaded, 6 * 16)
            dve.wait_ge(rows_loaded, 32)
            high_low(w3h[:, :, :].rearrange("p a b -> p (a b)"), w3l[:, :, :].rearrange("p a b -> p (a b)"), st_w3)
            for br in range(BR):
                cols = st_w2[:, br * SHIFTS * P:(br + 1) * SHIFTS * P].rearrange("p (a o) -> p a o", o=CH)
                scale = st_s2[:, br * CH:(br + 1) * CH].unsqueeze(1).to_broadcast([P, 2 * SHIFTS, CH])
                ins = nc.vector.tensor_tensor(cols, cols, scale, ALU.mult)
            then(ins)
            high_low(w2h[:, :, :].rearrange("p a b -> p (a b)"), w2l[:, :, :].rearrange("p a b -> p (a b)"), st_w2)
            nc.vector.tensor_scalar(c3T[0:KM - 1, :], c3T[0:KM - 1, :], vec[0:KM - 1, V_AL:V_AL + 1], None, ALU.mult)

            def fused_bias(dst, s, b, bb):
                nc.vector.scalar_tensor_tensor(der[:, dst:dst + 1], vec[:, b:b + 1], vec[:, s:s + 1],
                                               vec[:, bb:bb + 1], ALU.mult, ALU.add)

            fused_bias(D_H, V_S1, V_B1, V_BB1)
            fused_bias(D_A, V_S2, V_B2, V_BB2)
            fused_bias(D_M, V_SM, V_BM, V_BBM)
            fused_bias(D_B, V_SO, V_BO, V_BBO)
            nc.vector.tensor_tensor(der[:, D_D:D_D + 1], vec[:, V_C1:V_C1 + 1], vec[:, V_C2:V_C2 + 1],
                                    ALU.subtract).then_inc(setup_done, 1)

            def mean(n, h, r):
                dve.wait_ge(x_loaded[r], h * 32 + 32)
                nc.vector.tensor_reduce(xm[:, :, :], xb[r][:, :, :].rearrange("p c (t v) -> p c v t", v=V),
                                        AX.X, ALU.add).then_inc(xm_ready, 1)

            def differences(n):
                dve.wait_ge(tr_full[1], n * TRB + G_PROJ // 2 + 1)
                nc.vector.tensor_copy(proj2[:, :], ps_tr[1][0:SUB * REL, 0:V]).then_inc(tr_taken[1], 1)
                dve.wait_ge(tr_taken[1], n * TRB + G_PROJ // 2 + 1)
                nc.vector.tensor_tensor(diff[:, :].rearrange("r (u v) -> r u v", v=V),
                                        ps_tr[0][0:SUB * REL, 0:V].unsqueeze(2).to_broadcast([SUB * REL, V, V]),
                                        proj2[:, :].unsqueeze(1).to_broadcast([SUB * REL, V, V]),
                                        ALU.subtract).then_inc(tr_taken[0], 1)

            def take_tr(n, k, js=range(7)):
                for j in js:
                    t0 = HCH[k][0] + 4 * j
                    g = TR_OF[k] + j
                    if g % 2:
                        dve.wait_ge(tr_full[1], n * TRB + g // 2 + 1)
                        nc.vector.tensor_copy(inpT[0:KP, :, t0:t0 + 4],
                                              ps_tr[1][0:KP, :].rearrange("k (t p) -> k p t", t=4)
                                              ).then_inc(tr_taken[1], 1)

            def take_top(n, j):
                g = G_TOP + j
                us = min(UPG, V - j * UPG)
                dve.wait_ge(tr_full[g % 2], n * TRB + g // 2 + 1)
                nc.vector.tensor_copy(
                    top[0:KP, 0:P * 2 * V].rearrange("k (p c u) -> k u c p", c=2, u=V)[:, j * UPG:j * UPG + us],
                    ps_tr[g % 2][0:KP, 0:us * 2 * P].rearrange("k (u c p) -> k u c p", c=2, u=us)
                ).then_inc(tr_taken[g % 2], 1)

            def add_x(m, k, cb, buf):
                u0, us = UCH[k]
                y = ps_y[cb][:, 0:us * T].rearrange("c (u t) -> c u t", t=T)
                dve.wait_ge(y_full[cb], m * NK + k + 1)
                nc.vector.scalar_tensor_tensor(y, y, vec[:, V_GB + cb:V_GB + cb + 1], joints(buf, 0, P, cb, u0, us),
                                               ALU.add, ALU.add).then_inc(y_added[cb], 1)

            def y_low(m, k, cb):
                w = UCH[k][1] * T
                dve.wait_ge(yh_ready[cb], m * NK + k + 1)
                nc.vector.scalar_tensor_tensor(yl[:, cb, 0:w], ps_y[cb][:, 0:w], 0.0, yh[:, cb, 0:w].bitcast(F32),
                                               ALU.max, ALU.subtract).then_inc(y_split[cb], 1)

            def both_added(m, k, buf):
                for cb in range(CB):
                    add_x(m, k, cb, buf)

            def both_low(m, k):
                for cb in range(CB):
                    y_low(m, k, cb)

            def h_high(m, k):
                us = UCH[k][1]
                dve.wait_ge(hf_ready, m * NK + k + 1)
                nc.vector.tensor_copy(hh[:, 0:us, :], hf[:, 0:us, :]).then_inc(hh_ready, 1)

            def pooled(m, k, buf, part=None):
                u0, us = UCH[k]
                low = ps_m[0:CH, 0:us * T].rearrange("c (u t) -> c u t", t=T)
                high = ps_m[CH:P, 0:us * T].rearrange("c (u t) -> c u t", t=T)
                if part != 1:
                    dve.wait_ge(mf_ready, m * NK + k + 1)
                    nc.vector.tensor_tensor(low, mf[:, 0:us, 0:T], mf[:, 0:us, 1:T + 1], ALU.max).then_inc(pool_step, 1)
                    nc.vector.scalar_tensor_tensor(high, high, vec[CH:P, V_SO:V_SO + 1],
                                                   joints(buf, CH, P, 1, u0, us), ALU.mult, ALU.add)
                if part != 0:
                    dve.wait_ge(pool_step, m * 2 * NK + 2 * k + 1)
                    nc.vector.tensor_tensor(low, low, mf[:, 0:us, 2:T + 2], ALU.max).then_inc(pool_step, 1)
                    dve.wait_ge(pool_step, m * 2 * NK + 2 * k + 2)
                    nc.vector.scalar_tensor_tensor(low, low, vec[0:CH, V_SO:V_SO + 1], joints(buf, 0, CH, 1, u0, us),
                                                   ALU.mult, ALU.add).then_inc(sumB_ready, 1)

            def convolved(m, k, buf):
                u0, us = UCH[k]
                dve.wait_ge(conv_full, m * NK + k + 1)
                if some(m * NK + k):
                    dve.wait_ge(outA_done, m * NK + k)
                for br in range(BR):
                    rows = slice(br * CH, (br + 1) * CH)
                    for pair in range(2):
                        got = ps_h[pair * CH:(pair + 1) * CH, br * BRW:br * BRW + us * Q[0]]
                        xj = joints(buf, br * CH, (br + 1) * CH, 0, u0, us)
                        if br == 0:
                            got = got.rearrange("c (u q) -> c u q", u=us)
                            xj = xj.rearrange("c u (q e) -> c e u q", e=2)[:, pair]
                        else:
                            got = got.rearrange("c (u s q) -> c u s q", u=us, s=2)
                            xj = xj.rearrange("c u (q e s) -> c e u s q", e=2, s=2)[:, pair]
                        ins = nc.vector.tensor_tensor(steps_of(sumA[rows, 0:us * T], br, pair), got, xj, ALU.add)
                ins.then_inc(sumA_ready, 1)

            def step(n, h, r, head, tail, ahead):
                m = n - 1
                buf = xb[(r - 1) % NX]
                h1, r1 = following(h, r)
                for k in range(3):
                    if head:
                        take_tr(n, k, range(5))
                    if tail and k:
                        h_high(m, k - 1)
                    if head:
                        take_tr(n, k, (5, 6))
                    if tail and k:
                        pooled(m, k - 1, buf, 0)
                    if tail:
                        both_added(m, k, buf)
                    if tail and k:
                        pooled(m, k - 1, buf, 1)
                    if tail:
                        both_low(m, k)
                    if tail and k:
                        convolved(m, k - 1, buf)
                if head:
                    take_tr(n, 3, range(5))
                if tail:
                    h_high(m, 2)
                if head:
                    take_tr(n, 3, (5, 6))
                if tail:
                    pooled(m, 2, buf, 0)
                    both_added(m, 3, buf)
                if head:
                    take_tr(n, 4, (0, 1))
                if tail:
                    both_low(m, 3)
                    pooled(m, 2, buf, 1)
                if head:
                    take_tr(n, 4, (2, 3))
                if tail:
                    convolved(m, 2, buf)
                if head:
                    take_top(n, 1)
                    take_top(n, 3)
                if tail:
                    both_added(m, 4, buf)
                if head:
                    take_top(n, 5)
                if tail:
                    h_high(m, 3)
                if head:
                    take_top(n, 7)
                if tail:
                    both_low(m, 4)
                    pooled(m, 3, buf)
                    convolved(m, 3, buf)
                    h_high(m, 4)
                    pooled(m, 4, buf)
                    convolved(m, 4, buf)
                if ahead:
                    mean(n + 1, h1, r1)
                    differences(n + 1)

            mean(0, 0, 0)
            differences(0)
            all_samples(dve, step)

        @block.tensor
        def _(pe):
            def three(out, w, a, first, last):
                nc.tensor.matmul(out, w[0], a[0], start=first, stop=False)
                nc.tensor.matmul(out, w[0], a[1], start=False, stop=False)
                return nc.tensor.matmul(out, w[1], a[0], start=False, stop=last)

            def s1_half(n, k, b, kb):
                w = HCH[k][1] * V
                if b == 0 and kb == 0:
                    pe.wait_ge(xl_ready, n * NK + k + 1)
                before = n * 3 * NK + 3 * k + b // 2
                if kb == 0 and some(before):
                    pe.wait_ge(inp_taken[b % 2], before)
                cols = slice(b * P, (b + 1) * P)
                ins = three(ps_inp[b % 2][:, 0:w], (rwh[:, kb, cols], rwl[:, kb, cols]),
                            (xh[k % 2][:, kb, 0:w], xl[k % 2][:, kb, 0:w]), kb == 0, kb == CB - 1)
                if kb == CB - 1:
                    ins.then_inc(inp_full[b % 2], 1)

            def s1(n, k, b):
                for kb in range(CB):
                    s1_half(n, k, b, kb)

            def tr1(n, k, j):
                g = TR_OF[k] + j
                if j == 0:
                    for b in range(2):
                        pe.wait_ge(inp_taken[b], n * 3 * NK + 3 * (k + 1))
                pe.wait_ge(tr_taken[g % 2], n * TRB + g // 2)
                for t in range(4):
                    ins = nc.tensor.transpose(ps_tr[g % 2][0:KP, t * P:(t + 1) * P], inp[k % 2][:, 4 * j + t, :],
                                              ident[:, :])
                ins.then_inc(tr_full[g % 2], 1)

            def projections(n):
                pe.wait_ge(xm_ready, n + 1)
                for s in range(2):
                    g = G_PROJ + s
                    if some(n * TRB):
                        pe.wait_ge(tr_taken[g % 2], n * TRB)
                    for kb in range(CB):
                        ins = nc.tensor.matmul(ps_tr[g % 2][0:SUB * REL, 0:V],
                                               c12T[:, kb, s * SUB * REL:(s + 1) * SUB * REL], xm[:, kb, :],
                                               start=kb == 0, stop=kb == CB - 1)
                    ins.then_inc(tr_full[g % 2], 1)

            def topologies(n, j):
                g = G_TOP + j
                if j == 0:
                    pe.wait_ge(tanh_ready, n + 1)
                pe.wait_ge(tr_taken[g % 2], n * TRB + g // 2)
                for uu in range(min(UPG, V - j * UPG)):
                    u = j * UPG + uu
                    for c in range(2):
                        w0 = u * MW + (KA if c == 0 else 0)
                        ins = nc.tensor.matmul(ps_tr[g % 2][0:KP, (2 * uu + c) * P:(2 * uu + c + 1) * P],
                                               mbd[:, w0:w0 + KP], c3T[:, c * P:(c + 1) * P],
                                               start=True, stop=True)
                ins.then_inc(tr_full[g % 2], 1)

            def s2(n, j):
                g = G_S2 + j
                if j == 0:
                    for b in range(2):
                        pe.wait_ge(tr_taken[b], n * TRB + groups_before(G_S2, b))
                else:
                    pe.wait_ge(tr_taken[g % 2], n * TRB + g // 2)
                for i in range(min(PPG, P - j * PPG)):
                    p = j * PPG + i
                    ins = nc.tensor.matmul(ps_tr[g % 2][:, i * SW:(i + 1) * SW], inpT[0:KP, p, :],
                                           top[0:KP, p * 2 * V:p * 2 * V + SW], start=True, stop=True)
                ins.then_inc(tr_full[g % 2], 1)

            def tr2(m, k):
                u0, us = UCH[k]
                if k == 0:
                    for b in range(2):
                        pe.wait_ge(tr_taken[b], m * TRB + TRB)
                for cb in range(CB):
                    if some(m * NK + k):
                        pe.wait_ge(y_split[cb], m * NK + k)
                    for j in range(us):
                        src = top[:, 0:P * 2 * V].rearrange("t (p c u) -> t c u p", c=2, u=V)[:, cb, u0 + j, :]
                        ins = nc.tensor.transpose(ps_y[cb][:, j * T:(j + 1) * T], src, ident[:, :])
                    ins.then_inc(y_full[cb], 1)

            def s3_half(m, k, blk, kb):
                w = UCH[k][1] * T
                if blk == 0 and kb == 0:
                    for cb in range(CB):
                        pe.wait_ge(y_split[cb], m * NK + k + 1)
                if kb == 0 and some(m * NK + k):
                    pe.wait_ge(outB_done if blk else sumA_ready, m * NK + k)
                cols = slice(blk * P, (blk + 1) * P)
                ins = three((ps_m if blk else ps_h)[:, 0:w], (w3h[:, kb, cols], w3l[:, kb, cols]),
                            (yh[:, kb, 0:w], yl[:, kb, 0:w]), kb == 0, kb == CB - 1)
                if kb == CB - 1:
                    ins.then_inc(m_full if blk else h_full, 1)

            S3 = ((0, 0), (0, 1), (1, 0), (1, 1))

            def conv(m, k, parts=range(BR * SHIFTS)):
                us = UCH[k][1]
                if 0 in parts:
                    pe.wait_ge(hl_ready, m * NK + k + 1)
                for part in parts:
                    br, shift = part // SHIFTS, part % SHIFTS
                    ins = three(ps_h[:, br * BRW:br * BRW + us * Q[0]], (w2h[:, part, :], w2l[:, part, :]),
                                (runs(hh[:, 0:us, :], br, shift), runs(hl[:, 0:us, :], br, shift)),
                                shift == 0, shift == SHIFTS - 1)
                if BR * SHIFTS - 1 in parts:
                    ins.then_inc(conv_full, 1)

            def step(n, h, r, head, tail, ahead):
                m = n - 1
                if head:
                    tr1(n, 0, 0)
                    for j, (k, b, kb) in enumerate(((1, 5, 0), (1, 5, 1), (2, 0, 0), (2, 0, 1), (2, 1, 0))):
                        s1_half(n, k, b, kb)
                        tr1(n, 0, j + 1)
                    tr1(n, 0, 6)
                    s1_half(n, 2, 1, 1)
                if tail:
                    tr2(m, 0)
                if head:
                    for b in range(2, BLK):
                        s1(n, 2, b)
                for k in range(1, 3):
                    if head:
                        tr1(n, k, 0)
                        s1_half(n, k + 2, 0, 0)
                        tr1(n, k, 1)
                    for j, half in enumerate(S3):
                        if tail:
                            s3_half(m, k - 1, *half)
                        if head:
                            tr1(n, k, j + 2)
                    if head:
                        tr1(n, k, 6)
                        s1_half(n, k + 2, 0, 1)
                        s1(n, k + 2, 1)
                    if tail:
                        tr2(m, k)
                    if head:
                        s1(n, k + 2, 2)
                        s1(n, k + 2, 3)
                    if tail:
                        conv(m, k - 1)
                    if head:
                        s1(n, k + 2, 4)
                        s1(n, k + 2, 5)
                if head:
                    tr1(n, 3, 0)
                    tr1(n, 3, 1)
                for j, half in enumerate(S3):
                    if tail:
                        s3_half(m, 2, *half)
                    if head:
                        tr1(n, 3, j + 2)
                if ahead:
                    s1_half(n + 1, 0, 0, 0)
                if head:
                    tr1(n, 3, 6)
                if ahead:
                    s1_half(n + 1, 0, 0, 1)
                if tail:
                    tr2(m, 3)
                if head:
                    tr1(n, 4, 0)
                    tr1(n, 4, 1)
                if tail:
                    conv(m, 2, (0, 1))
                if head:
                    tr1(n, 4, 2)
                if ahead:
                    s1(n + 1, 0, 1)
                if head:
                    tr1(n, 4, 3)
                if tail:
                    conv(m, 2, (2, 3, 4, 5))
                    tr2(m, 4)
                for j in range(N_TOP):
                    if head:
                        topologies(n, j)
                    if ahead and j in (1, N_TOP - 1):
                        s1(n + 1, 0, 2 if j == 1 else 3)
                    if tail and 3 <= j < 3 + len(S3):
                        s3_half(m, 3, *S3[j - 3])
                for j in range(N_S2):
                    if head:
                        s2(n, j)
                    if ahead:
                        for b in ahead_blocks(j):
                            s1(n + 1, b // BLK, b % BLK)
                    if tail and j == 2:
                        conv(m, 3)
                    if tail and j == 4:
                        for half in S3[:2]:
                            s3_half(m, 4, *half)
                    if tail and j == 6:
                        for half in S3[2:]:
                            s3_half(m, 4, *half)
                    if tail and j == 9:
                        conv(m, 4)
                if ahead:
                    projections(n + 1)
                    s1(n + 1, 1, 4)

            pe.wait_ge(rw_split, 1)
            for b in range(AHEAD_S2):
                s1(0, b // BLK, b % BLK)
            pe.wait_ge(setup_done, 1)
            projections(0)
            s1(0, 1, 4)
            all_samples(pe, step)


def kernel(**a):
    import numpy as np
    import concourse.bacc as bacc
    from concourse.bass_utils import run_bass_kernel_spmd

    a = {k.replace("L0_conv_", ""): np.asarray(v) for k, v in a.items()}
    N, C = a["x"].shape[:2]
    f = np.float32
    z64 = np.zeros(64, f)

    def kblocks(w):
        return np.ascontiguousarray(w.reshape(CB, P, -1).transpose(1, 0, 2).reshape(P, -1))

    rw = a["g_rw"].reshape(SUB, CB, P, C).transpose(3, 1, 0, 2).reshape(C, BLK * P)
    w3 = np.concatenate([a["br_w1"].reshape(2 * 64, C), a["mp_w1"], a["p_w"]], 0).T
    w2 = np.zeros((2, CH, BR, SHIFTS, 2, CH), f)
    for shift in range(SHIFTS):
        for i in range(2):
            for o in range(2):
                tap = 2 * (shift - 1) + i - o + KS // 2
                if 0 <= tap < KS:
                    w2[i, :, :, shift, o, :] = a["br_w2"][:, :, :, tap].transpose(2, 0, 1)
    c12 = np.concatenate([a["g_c1w"].reshape(SUB * REL, C), a["g_c2w"].reshape(SUB * REL, C)], 0).T
    c3 = np.concatenate([a["g_c3w"].transpose(0, 2, 1).reshape(SUB * REL, C), a["g_c3b"], np.ones((1, C), f)], 0)
    atop = np.ascontiguousarray(a["A"].transpose(1, 0, 2)).reshape(1, V, KA)
    ind = np.ascontiguousarray(np.broadcast_to(np.repeat(np.eye(SUB, dtype=f), V, 1)[:, None, :], (SUB, V, KA)))
    vecs = np.zeros((P, NV), f)
    vecs[:, V_GS:V_GS + 2] = a["gbn_s"].reshape(CB, P).T
    vecs[:, V_GB:V_GB + 2] = a["gbn_b"].reshape(CB, P).T
    vecs[:, V_RB:V_RB + 6] = a["g_rb"].reshape(SUB, CB, P).transpose(2, 1, 0).reshape(P, BLK)
    for col, v in ((V_S1, a["br_s1"].reshape(P)), (V_B1, a["br_b1"].reshape(P)), (V_BB1, a["br_bb1"].reshape(P)),
                   (V_S2, a["br_s2"].reshape(P)), (V_B2, a["br_b2"].reshape(P)), (V_BB2, a["br_bb2"].reshape(P)),
                   (V_SM, np.concatenate([a["mp_s1"], z64])), (V_BM, np.concatenate([a["mp_b1"], z64])),
                   (V_BBM, np.concatenate([a["mp_bb1"], z64])), (V_SO, np.concatenate([a["mp_s2"], a["p_s"]])),
                   (V_BO, np.concatenate([z64, a["p_b"]])), (V_BBO, np.concatenate([a["mp_bb2"], a["p_bb"]]))):
        vecs[:, col] = v
    vecs[0:SUB * REL, V_C1] = a["g_c1b"].reshape(-1)
    vecs[0:SUB * REL, V_C2] = a["g_c2b"].reshape(-1)
    vecs[:, V_AL] = a["alpha"][0]
    arrays = {
        "x": np.ascontiguousarray(a["x"].reshape(N, C, TV)), "rw": kblocks(rw), "c12": kblocks(c12), "c3": c3,
        "atop": atop, "ind": ind, "w3": kblocks(w3), "w2": w2.reshape(P, BR * SHIFTS * P),
        "s2row": np.ascontiguousarray(a["br_s2"].reshape(P)), "ident": np.eye(P, dtype=f), "vecs": vecs,
    }
    nc = bacc.Bacc("TRN2", target_bir_lowering=False, num_devices=1,
                   dynamic_dma_scratch_size=1024)
    args, ins = [], {}
    for name, arr in arrays.items():
        arr = np.ascontiguousarray(arr)
        ins[f"in_{name}"] = arr
        args.append(nc.dram_tensor(f"in_{name}", arr.shape, mybir.dt.from_np(arr.dtype), kind="ExternalInput").ap())
    args.append(nc.dram_tensor("out", (N, C, TV), F32, kind="ExternalOutput").ap())
    args[2] = args[2].rearrange("p (k o) -> p k o", k=CB)
    build(nc, *args)
    r = run_bass_kernel_spmd(nc, [ins], core_ids=[0])
    return r.results[0]["out"].reshape(N, C, T, V)
```
